# Optimizing a Trainium2 kernel written in Bass

```python
import numpy as np
import jax
import jax.numpy as jnp

def _softmax(x, axis=-1):
    return jax.nn.softmax(x, axis=axis)

def _gelu(x):
    return jax.nn.gelu(x, approximate=True)

def _silu(x):
    return jax.nn.silu(x)

def _sigmoid(x):
    return jax.nn.sigmoid(x)

def _layernorm(x, axis=-1, eps=1e-05):
    m = jnp.mean(x, axis=axis, keepdims=True)
    v = jnp.var(x, axis=axis, keepdims=True)
    return (x - m) / jnp.sqrt(v + eps)

def _scatter_add(tgt, idx, src, axis=0):
    return tgt.at[idx].add(src)

def _segment_sum(src, seg, n):
    return jax.ops.segment_sum(src, seg, n)
kernel_name = 'mk_seq_preln_d1_jaxref_r8_46ca5b'

def setup_inputs(seed: int=0):
    np.random.seed(seed)
    _w = jnp.asarray

    def _L0_attn_setup():
        import jax, jax.numpy as jnp
        import numpy as np
        D_MODEL = 128
        N_HEADS = 16
        D_HIDDEN = 512
        BATCH = 2
        N_CTX = 256

        def _split_heads(t, n_heads):
            B, S, D = t.shape
            return t.reshape(B, S, n_heads, D // n_heads).transpose(0, 2, 1, 3)
        key = jax.random.key(seed)
        ks = jax.random.split(key, 4)
        scale = 0.02
        x = jax.random.normal(ks[0], (BATCH, N_CTX, D_MODEL), dtype=jnp.float32)
        Wk = jax.random.normal(ks[1], (D_MODEL, D_MODEL), dtype=jnp.float32) * scale
        bk = jnp.zeros((D_MODEL,), dtype=jnp.float32)
        Wv = jax.random.normal(ks[2], (D_MODEL, D_HIDDEN), dtype=jnp.float32) * scale
        bv = jnp.zeros((D_HIDDEN,), dtype=jnp.float32)
        Wf = jax.random.normal(ks[3], (D_HIDDEN, D_MODEL), dtype=jnp.float32) * scale
        bf = jnp.zeros((D_MODEL,), dtype=jnp.float32)
        return {'x': x, 'Wk': Wk, 'bk': bk, 'Wv': Wv, 'bv': bv, 'Wf': Wf, 'bf': bf}
    _L0_attn_in = _L0_attn_setup()

    def _L0_ffn_setup():
        import jax, jax.numpy as jnp
        import numpy as np
        B, N, DIM = (2, 256, 128)
        HEADS, DIM_HEAD, EXPERTS = (8, 64, 8)
        SCALE = DIM_HEAD ** (-0.5)
        key = jax.random.key(seed)
        ks = jax.random.split(key, 6)
        dim_inner = HEADS * DIM_HEAD
        return {'x': jax.random.normal(ks[0], (B, N, DIM), jnp.float32), 'w_q': jax.random.normal(ks[1], (DIM, dim_inner), jnp.float32) * 0.02, 'w_k': jax.random.normal(ks[2], (DIM, dim_inner), jnp.float32) * 0.02, 'w_gate': jax.random.normal(ks[3], (DIM, HEADS * EXPERTS), jnp.float32) * 0.02, 'value_experts': jax.random.normal(ks[4], (EXPERTS, HEADS, DIM, DIM_HEAD), jnp.float32) * 0.02, 'output_experts': jax.random.normal(ks[5], (EXPERTS, HEADS, DIM_HEAD, DIM), jnp.float32) * 0.02}
    _L0_ffn_in = _L0_ffn_setup()
    _d = {'L0_attn_x': _L0_attn_in['x'], 'L0_attn_Wk': _L0_attn_in['Wk'], 'L0_attn_bk': _L0_attn_in['bk'], 'L0_attn_Wv': _L0_attn_in['Wv'], 'L0_attn_bv': _L0_attn_in['bv'], 'L0_attn_Wf': _L0_attn_in['Wf'], 'L0_attn_bf': _L0_attn_in['bf'], 'L0_ffn_w_q': _L0_ffn_in['w_q'], 'L0_ffn_w_k': _L0_ffn_in['w_k'], 'L0_ffn_w_gate': _L0_ffn_in['w_gate'], 'L0_ffn_value_experts': _L0_ffn_in['value_experts'], 'L0_ffn_output_experts': _L0_ffn_in['output_experts']}
    _x0 = _d['L0_attn_x']
    _d['L0_attn_x'] = jax.random.normal(jax.random.fold_in(jax.random.key(seed), 1), (8, 512, 128), dtype=_x0.dtype)
    del _x0
    return _d

def reference(L0_attn_x, L0_attn_Wk, L0_attn_bk, L0_attn_Wv, L0_attn_bv, L0_attn_Wf, L0_attn_bf, L0_ffn_w_q, L0_ffn_w_k, L0_ffn_w_gate, L0_ffn_value_experts, L0_ffn_output_experts):

    def _L0_attn_ref(x, Wk, bk, Wv, bv, Wf, bf):
        import jax, jax.numpy as jnp
        import numpy as np
        D_MODEL = 128
        N_HEADS = 16
        D_HIDDEN = 512
        BATCH = 2
        N_CTX = 256

        def _split_heads(t, n_heads):
            B, S, D = t.shape
            return t.reshape(B, S, n_heads, D // n_heads).transpose(0, 2, 1, 3)
        B, S, D = x.shape
        H = N_HEADS
        Q = _split_heads(x, H)
        K = _split_heads(x @ Wk + bk, H)
        V = _split_heads(x @ Wv + bv, H)
        causal = jnp.tril(jnp.ones((S, S), dtype=bool))
        mask = jnp.where(causal, 0.0, -jnp.inf).astype(x.dtype)
        scores = jnp.einsum('bhqd,bhkd->bhqk', Q, K) + mask
        attn = jax.nn.softmax(scores, axis=-1)
        o = jnp.einsum('bhqk,bhkd->bhqd', attn, V)
        o = o.transpose(0, 2, 1, 3).reshape(B, S, -1)
        return x + jax.nn.gelu(o, approximate=False) @ Wf + bf

    def _L0_ffn_ref(x, w_q, w_k, w_gate, value_experts, output_experts):
        import jax, jax.numpy as jnp
        import numpy as np
        B, N, DIM = (2, 256, 128)
        HEADS, DIM_HEAD, EXPERTS = (8, 64, 8)
        SCALE = DIM_HEAD ** (-0.5)
        b, n, _ = x.shape
        q = (x @ w_q).reshape(b, n, HEADS, DIM_HEAD).transpose(0, 2, 1, 3)
        k = (x @ w_k).reshape(b, n, HEADS, DIM_HEAD).transpose(0, 2, 1, 3)
        gates = jax.nn.sigmoid((x @ w_gate).reshape(b, n, HEADS, EXPERTS).transpose(0, 2, 1, 3))
        sel = jnp.argmax(gates, axis=-1)
        gm = jax.nn.one_hot(sel, EXPERTS, dtype=x.dtype) * gates
        values = jnp.einsum('bhne,ehdk,bnd->bhnk', gm, value_experts, x)
        sim = jnp.einsum('bhid,bhjd->bhij', q * SCALE, k)
        causal_mask = jnp.triu(jnp.ones((n, n), dtype=bool), 1)
        sim = jnp.where(causal_mask, jnp.finfo(sim.dtype).min, sim)
        attn = jax.nn.softmax(sim, axis=-1)
        out = jnp.einsum('bhij,bhjk->bhik', attn, values)
        out = jnp.einsum('bhne,ehkd,bhnk->bhnd', gm, output_experts, out)
        return out.sum(axis=1)
    x = L0_attn_x
    x = x + _L0_attn_ref(_layernorm(x, axis=-1), L0_attn_Wk, L0_attn_bk, L0_attn_Wv, L0_attn_bv, L0_attn_Wf, L0_attn_bf)
    x = x + _L0_ffn_ref(_layernorm(x, axis=-1), L0_ffn_w_q, L0_ffn_w_k, L0_ffn_w_gate, L0_ffn_value_experts, L0_ffn_output_experts)
    return x

_drawn_inputs = setup_inputs


def setup_inputs(seed=0):
    import zlib

    import numpy as np

    out = dict(_drawn_inputs(seed))
    spreads = {'L0_attn_bk': (0.0, 0.8), 'L0_attn_bv': (0.0, 0.738), 'L0_attn_bf': (0.0, 0.1)}
    factors = {'L0_attn_Wk': 8.0,
     'L0_attn_Wv': 8.0,
     'L0_attn_Wf': 5.086,
     'L0_ffn_w_q': 8.0,
     'L0_ffn_w_k': 8.0,
     'L0_ffn_w_gate': 8.0,
     'L0_ffn_value_experts': 8.0,
     'L0_ffn_output_experts': 8.0}
    for name, (base, spread) in spreads.items():
        noise = np.random.default_rng([zlib.crc32(name.encode()), seed]).standard_normal(out[name].shape)
        drawn = base * np.exp(spread * noise) if base else spread * noise
        out[name] = jnp.asarray(drawn.astype(out[name].dtype))
    for name, factor in factors.items():
        out[name] = (out[name] * factor).astype(out[name].dtype)
    return out
```

```python
import concourse.bass as bass
from concourse import mybir
from contextlib import ExitStack

F32 = mybir.dt.float32
F32R = mybir.dt.float32r
BF16 = mybir.dt.bfloat16
U32 = mybir.dt.uint32
ALU = mybir.AluOpType
ACT = mybir.ActivationFunctionType
AX = mybir.AxisListType

B, S, D = 8, 512, 128
P = 128
T = S // P
E = 8
HEADS = {"A": 16, "F": 8}
DV = {"A": 32, "F": 64}
GROUPS = 4
HG = {k: HEADS[k] // GROUPS for k in "AF"}
STAGES = 3
UNITS = {k: GROUPS * STAGES * HG[k] for k in "AF"}
NST = GROUPS * STAGES
DH = D // HEADS["A"]
PARTS = 3
STACK = PARTS * PARTS * DH
KROWS = 96
NEG = -3.0e38
EPS = 1e-5
SCALE = 0.125
RESTACK = {"A": 2 * PARTS * PARTS + 1, "F": 2}
WRITES = 2 * PARTS
MROWS = {"A": PARTS, "F": 2}

ORDER = ([("F", "xT", 0), ("F", "gate", 0)] + [("F", "qk", u) for u in range(8)]
         + [("F", "moe1", u) for u in range(T * E)] + [("F", "gmT", 0)]
         + [("F", "T", g) for g in range(GROUPS)]
         + [("A", "xT", 0), ("A", "K", 0)] + [("A", "V", t) for t in range(T)]
         + [("F", "moe2", u) for u in range(T * E)] + [("F", "out", 0)]
         + [("A", "T", g) for g in range(GROUPS)] + [("A", "W", 0)])
BANK = {name: n % 2 for n, name in enumerate(ORDER)}


def build(nc, x, wk, bk, wv, bv, wf, bf, wq, wkf, wg, ve, oe, ident, consts, out):
    ctx = ExitStack()
    with ctx:
        def sb(name, shape, dt=F32):
            return ctx.enter_context(nc.sbuf_tensor(name, shape, dt))

        sems = []

        def sem(name):
            sems.append(ctx.enter_context(nc.semaphore(name)))
            return sems[-1]

        wk_h, wk_l = sb("wk_h", [P, D], F32R), sb("wk_l", [P, D], F32R)
        wv_h, wv_l = sb("wv_h", [P, S], F32R), sb("wv_l", [P, S], F32R)
        wq_h, wq_l = sb("wq_h", [P, S], F32R), sb("wq_l", [P, S], F32R)
        wkf_h, wkf_l = sb("wkf_h", [P, S], F32R), sb("wkf_l", [P, S], F32R)
        wg_h, wg_l = sb("wg_h", [P, 64], F32R), sb("wg_l", [P, 64], F32R)
        ve_h, ve_l = sb("ve_h", [P, E, S], F32R), sb("ve_l", [P, E, S], F32R)
        oe_sb = sb("oe_sb", [P, 4 * E, D])
        wf_sb = sb("wf_sb", [P, GROUPS, D])
        spread = sb("spread", [P, 4 * E, P], F32R)
        ident_sb = sb("ident_sb", [P, P])
        ident_b = sb("ident_b", [P, P], BF16)
        ident2 = sb("ident2", [P, 64])
        ones = sb("ones", [P, 64])
        mask = sb("mask", [P, S], BF16)
        bk_sb = sb("bk_sb", [P, 1])
        bv_sb = sb("bv_sb", [P, S])
        bf_sb = sb("bf_sb", [P, D])
        rank = sb("rank", [P, E])
        half = sb("half", [P, T])
        x_sb = sb("x_sb", [P, T, D])
        xn = {k: sb(f"xn{k}", [P, T, D]) for k in "AF"}
        x1 = sb("x1", [P, T, D])
        xh, xl = sb("xh", [P, S], F32R), sb("xl", [P, S], F32R)
        s1q, s1k = sb("s1q", [P, 8, S], F32R), sb("s1k", [P, 8, S], F32R)
        s2q, s2k = sb("s2q", [P, 8, S], F32R), sb("s2k", [P, 8, S], F32R)
        qs = s1q[:].rearrange("p a b -> p (a b)").bitcast(BF16).rearrange("p (h n) -> p h n", n=S)
        ks = s2k[:].rearrange("p a b -> p (a b)").bitcast(BF16).rearrange("p (h n) -> p h n", n=S)
        val = sb("val", [P, T, S])
        osb = sb("osb", [P, GROUPS, S])
        pt = sb("pt", [P, 8, S])
        at = sb("at", [P, 2, S])
        gmt = sb("gmt", [P, S], F32R)
        junk = sb("junk", [P, 2, S], BF16)
        mx = sb("mx", [P, 2, 16])
        nm_r = sb("nm_r", [P, 2, 16])
        nm_a = sb("nm_a", [P, 2, 48], BF16)
        nm_f = sb("nm_f", [P, 2, 16])
        mt_a = sb("mt_a", [48, 2, P], BF16)
        mt_f = sb("mt_f", [16, 2, P])
        st = sb("st", [P, T, 6])
        mv = sb("mv", [P, T, 2])
        veps, rstd = sb("veps", [P, T]), sb("rstd", [P, T])
        gmax, wmax = sb("gmax", [P, T * 8]), sb("wmax", [P, T * 8])
        gflat = osb[:].rearrange("p a b -> p (a b)")
        g_s, g_w, g_m = gflat[:, 0:256], gflat[:, 256:512], gflat[:, 512:768]
        hot = gflat[:, 768:1024].bitcast(U32)
        g_t = gflat[:, 1024:1536].rearrange("p (t c) -> p t c", c=P)

        def part(n):
            return pt[:, n // 2, :].bitcast(BF16)[:, (n % 2) * S:(n % 2) * S + S]

        def by_head(ap):
            return ap.rearrange("p (a e) -> p a e", e=E)

        def bank(name):
            return ctx.enter_context(nc.psum_tensor(name, [P, S], F32))
        ps_max = [bank("ps_max0"), bank("ps_max1")]
        ps_exp = [bank("ps_exp0"), bank("ps_exp1")]
        ps_o, ps_d = bank("ps_o"), bank("ps_d")
        ps_m = [bank("ps_m0"), bank("ps_m1")]

        parts_d = {n: nc.dram_tensor(f"parts_{n}", (PARTS, P, S), BF16).ap() for n in "qk"}
        zeros_d = nc.dram_tensor("zeros_d", (4, 4096), F32).ap()
        ones_d = nc.dram_tensor("ones_d", (2, 4096), F32).ap()
        onesb_d = nc.dram_tensor("onesb_d", (PARTS, 8192), BF16).ap()

        w_in = [sem(f"w_in{n}") for n in range(3)]
        split_hi, split_lo = sem("split_hi"), sem("split_lo")
        set_v, set_p = sem("set_v"), sem("set_p")
        cst = sem("cst")
        cleared = {n: sem(f"cleared_{n}") for n in ("sp", "pe", "act", "pool", "dve")}
        first_of_batch = len(sems)
        arrived = sem("arrived")
        x_in = sem("x_in")
        K2 = lambda n: {k: sem(f"{n}{k}") for k in "AF"}
        ln_st, ln_mv, ln_ve, ln_rs, ln_xn = (K2(n) for n in ("ln_st", "ln_mv", "ln_ve", "ln_rs", "ln_xn"))
        xt_ready, xh_done, xl_done = K2("xt_ready"), K2("xh_done"), K2("xl_done")
        restacked = K2("restacked")
        pair_sent = [sem("pair_sent0"), sem("pair_sent1")]
        max_ready, max_done = K2("max_ready"), K2("max_done")
        neg_step, neg_ready = K2("neg_step"), K2("neg_ready")
        t_ready, t_done = K2("t_ready"), K2("t_done")
        mrow = {k: [sem(f"mrow{k}{n}") for n in range(2)] for k in "AF"}
        s_ready, exp_done = K2("s_ready"), K2("exp_done")
        causal, pv_done, recip, o_done = K2("causal"), K2("pv_done"), K2("recip"), K2("o_done")
        q1, q_r, q2, q3 = sem("q1"), sem("q_r"), sem("q2"), sem("q3")
        k_ready, kf, k1, k_r, k2, k3 = (sem(n) for n in ("k_ready", "kf", "k1", "k_r", "k2", "k3"))
        parts_out = sem("parts_out")
        v_ready, va = sem("v_ready"), sem("va")
        resid = sem("resid")
        gelu_done, w_ready, x1_done = sem("gelu_done"), sem("w_ready"), sem("x1_done")
        gate_ready, gate_exp, gate_step, gt_ready, gmt_done = (
            sem(n) for n in ("gate_ready", "gate_exp", "gate_step", "gt_ready", "gmt_done"))
        gt_made, gt_half = sem("gt_made"), sem("gt_half")
        qk_ready, qk_hi, qk_lo = sem("qk_ready"), sem("qk_hi"), sem("qk_lo")
        moe1_ready, chosen, vf = sem("moe1_ready"), sem("chosen"), sem("vf")
        sp_ready, at_done, at_used = sem("sp_ready"), sem("at_done"), sem("at_used")
        acc_copied, out_ready, y_done, y_out = (sem(n) for n in ("acc_copied", "out_ready", "y_done", "y_out"))

        numbers = [s.num for s in sems[first_of_batch:]]
        per_batch = range(numbers[0], numbers[-1] + 1)
        assert numbers == list(per_batch)

        block = ctx.enter_context(nc.Block())
        GS = 8

        def each_batch(name, eng, first, body, last):
            def meet():
                eng.drain().then_inc(arrived, 1)
                if name == "sp":
                    eng.wait_ge(arrived, 5)
                    eng.sem_clear(per_batch)
                    for go in cleared.values():
                        eng.sem_inc(go, 1)
                eng.wait_ge(cleared[name], 1)
                eng.sem_clear(cleared[name])
            first(0)
            meet()
            with eng.Fori(0, B - 1) as i:
                body(i)
                meet()
            last(B - 1)

        @block.sync
        def _(sp):
            sp.dma_start(x_sb[:], x[0].rearrange("(t p) d -> p t d", p=P)).then_inc(x_in, 16)
            o = gflat
            sp.dma_start(ident_sb[:], ident).then_inc(w_in[0], 16)
            sp.dma_start(ident2[0:64, :], ident[0:64, 0:64]).then_inc(w_in[0], 16)
            sp.dma_start(ident2[64:128, :], ident[0:64, 0:64]).then_inc(w_in[0], 16)
            sp.dma_start(o[:, 0:128], wk).then_inc(w_in[0], 16)
            sp.dma_start(o[:, 128:640], wv).then_inc(w_in[0], 16)
            sp.dma_start(o[:, 640:1152], wq).then_inc(w_in[0], 16)
            sp.dma_start(o[:, 1152:1664], wkf).then_inc(w_in[0], 16)
            sp.dma_start(o[:, 1664:1728], wg).then_inc(w_in[0], 16)
            sp.dma_start(bk_sb[:], bk.rearrange("(p o) -> p o", o=1)).then_inc(w_in[1], 16)
            sp.dma_start(bv_sb[:], bv.partition_broadcast(P)).then_inc(w_in[1], 16)
            sp.dma_start(bf_sb[:], bf.partition_broadcast(P)).then_inc(w_in[1], 16)
            sp.dma_start(wf_sb[:], wf.rearrange("p (g d) -> p g d", d=D)).then_inc(w_in[1], 16)
            sp.dma_start(pt[:], ve.rearrange("p (e n) -> p e n", n=S)).then_inc(w_in[2], 16)
            sp.dma_start(oe_sb[:], oe.rearrange("p (c d) -> p c d", d=D)).then_inc(w_in[2], 16)
            sp.wait_ge(set_v, 5)
            sp.dma_start(zeros_d, s2q[0:4].bitcast(F32).rearrange("p a b -> p (a b)")).then_inc(cst, 16)
            sp.dma_start(ones_d, consts[0:2]).then_inc(cst, 16)
            sp.dma_start(onesb_d, consts[2:5].bitcast(BF16)).then_inc(cst, 16)
            sp.wait_ge(cst, 48)
            sp.dma_start(ks[STACK:STACK + PARTS], onesb_d.rearrange("p (h n) -> p h n", n=S)).then_inc(cst, 16)
            sp.wait_ge(cst, 64)

            def parts_to_dram(a):
                for n, (name, ready) in enumerate((("q", (q1, q2, q3)), ("k", (k1, k2, k3)))):
                    for m in range(PARTS):
                        sp.wait_ge(ready[m], a + 1)
                        sp.dma_start(parts_d[name][m], part(n * PARTS + m)).then_inc(parts_out, 16)

            def restack_a(a):
                sp.wait_ge(parts_out, (a + 1) * (16 * WRITES))
                for m in range(PARTS):
                    for n in range(PARTS):
                        r = (m * PARTS + n) * DH
                        sp.dma_start(qs[r:r + DH], parts_d["q"][m].rearrange("(h d) n -> d h n", d=DH)
                                     ).then_inc(restacked["A"], 16)
                        sp.dma_start(ks[r:r + DH], parts_d["k"][n].rearrange("(h d) n -> d h n", d=DH)
                                     ).then_inc(restacked["A"], 16)
                sp.dma_start(qs[STACK:STACK + PARTS],
                             zeros_d[0:3].bitcast(BF16).rearrange("p (h n) -> p h n", n=S)
                             ).then_inc(restacked["A"], 16)

            def restack_f(f):
                sp.dma_start(s2q[64:66].bitcast(F32), zeros_d[0:2].rearrange("p (h n) -> p h n", n=S)
                             ).then_inc(restacked["F"], 16)
                sp.dma_start(s2k[64:66].bitcast(F32), ones_d.rearrange("p (h n) -> p h n", n=S)
                             ).then_inc(restacked["F"], 16)
                for p in range(4):
                    sp.wait_ge(qk_lo, f * 8 + 2 * p + 2)
                    qh, ql, kh, kl = (pt[:, 4 * (p % 2) + n, :] for n in range(4))
                    for ab in range(2):
                        r, h = slice(64 * ab, 64 * ab + 64), 2 * p + ab
                        for dst, src in ((s1q[0:64, h], qh), (s1q[64:128, h], ql), (s1k[0:64, h], kh),
                                         (s1k[64:128, h], kh), (s2q[0:64, h], qh), (s2k[0:64, h], kl)):
                            sp.dma_start(dst.bitcast(F32), src[r]).then_inc(pair_sent[p % 2], 16)

            def maxima_rows(k, b):
                for g in range(GROUPS):
                    sp.wait_ge(t_done[k], b * GROUPS + g + 1)
                    for m in range(MROWS[k]):
                        if k == "A":
                            dst, src = qs[STACK + m:STACK + m + 1, 4 * g:4 * g + 4], mt_a[16 * m:16 * m + 16, g % 2]
                        else:
                            dst = s2q[64 + m:65 + m, 2 * g:2 * g + 2].bitcast(F32)
                            src = mt_f[8 * m:8 * m + 8, g % 2]
                        sp.dma_start(dst.rearrange("o h (t n) -> o (h t) n", n=P), src).then_inc(mrow[k][g % 2], 16)

            def attention(a):
                maxima_rows("A", a)

            def first(a, beside=False):
                parts_to_dram(a)
                restack_a(a)
                attention(a)

            def experts(f):
                restack_f(f)
                maxima_rows("F", f)

            def store(i, f=0):
                sp.wait_ge(y_done, f + 1)
                dst = out[i] if isinstance(i, int) else out[bass.ds(i, 1)].rearrange("o s d -> (o s) d")
                sp.dma_start(dst.rearrange("(t p) d -> p t d", p=P), xn["F"][:]).then_inc(y_out, 16)
                sp.wait_ge(y_out, 16)

            def body(i, f=0, a=0, beside=True):
                sp.dma_start(x_sb[:], x[bass.ds(i + 1, 1)].rearrange("o (t p) d -> p (o t) d", p=P)).then_inc(x_in, 16)
                experts(f)
                parts_to_dram(a)
                sp.wait_ge(s_ready["F"], (f + 1) * UNITS["F"])
                restack_a(a)
                store(i)
                attention(a)

            def last(i, f=0):
                experts(f)
                store(i)
            each_batch("sp", sp, first, body, last)

        @block.tensor
        def _(pe):
            mm = nc.tensor.matmul

            def mm3(dst, lh, ll, rh, rl):
                mm(dst, lh, rh, start=True, stop=False)
                mm(dst, ll, rh, start=False, stop=False)
                return mm(dst, lh, rl, start=False, stop=True)

            def free(banks, k, name, n, drained):
                b = BANK[(k, name, n)]
                if banks[b] is not None:
                    pe.wait_ge(*banks[b])
                banks[b] = drained
                return ps_m[b]

            def transposed(banks, k, b):
                dst = free(banks, k, "xT", 0, (xl_done[k], b + 1))
                pe.wait_ge(ln_xn[k], (b + 1) * T)
                for t in range(T):
                    last = nc.tensor.transpose(dst[:, t * P:t * P + P], xn[k][:, t, :], ident_sb[:])
                last.then_inc(xt_ready[k], 1)
                pe.wait_ge(xl_done[k], b + 1)

            def project_a(banks, a):
                transposed(banks, "A", a)
                dst = free(banks, "A", "K", 0, (kf, a + 1))
                mm3(dst[:], wk_h[:], wk_l[:], xh[:], xl[:]).then_inc(k_ready, 1)
                for t in range(T):
                    dst = free(banks, "A", "V", t, (va, a * T + t + 1))
                    r = slice(t * P, t * P + P)
                    mm3(dst[:], xh[:, r], xl[:, r], wv_h[:], wv_l[:]).then_inc(v_ready, 1)

            def project_f(banks, f):
                transposed(banks, "F", f)
                dst = free(banks, "F", "gate", 0, (gate_exp, f + 1))
                for t in range(T):
                    r = slice(t * P, t * P + P)
                    last = mm3(dst[:, t * 64:t * 64 + 64], xh[:, r], xl[:, r], wg_h[:], wg_l[:])
                last.then_inc(gate_ready, 1)
                for u in range(8):
                    wh, wl = ((wq_h, wq_l), (wkf_h, wkf_l))[u % 2]
                    c = slice(u // 2 * P, u // 2 * P + P)
                    dst = free(banks, "F", "qk", u, (qk_lo, f * 8 + u + 1))
                    mm3(dst[:], wh[:, c], wl[:, c], xh[:], xl[:]).then_inc(qk_ready, 1)

            def expert_values(banks, f):
                for t in range(T):
                    r = slice(t * P, t * P + P)
                    for e in range(E):
                        dst = free(banks, "F", "moe1", t * E + e, (chosen, f * (T * E) + t * E + e + 1))
                        mm3(dst[:], xh[:, r], xl[:, r], ve_h[:, e], ve_l[:, e]).then_inc(moe1_ready, 1)

            def gates_transposed(banks, f):
                dst = free(banks, "F", "gmT", 0, (gmt_done, f + 1))
                pe.wait_ge(gt_ready, f + 1)
                for t in range(T):
                    last = nc.tensor.transpose(dst[:, t * P:t * P + P], g_t[:, t, :], ident_sb[:])
                last.then_inc(gt_made, 1)

            def score(k, dst, h, rows, cols):
                (l1, l2), (r1, r2) = rows, cols
                if k == "A":
                    return mm(dst, l1[0:KROWS, h, l2], r1[0:KROWS, h, r2], start=True, stop=True)
                mm(dst, l1[0][:, h, l2], r1[0][:, h, r2], start=True, stop=False)
                return mm(dst, l1[1][0:KROWS, h, l2], r1[1][0:KROWS, h, r2], start=False, stop=True)

            Q = {"A": qs, "F": (s1q, s2q)}
            KK = {"A": ks, "F": (s1k, s2k)}

            def tile(n, m=1):
                return slice(n * P, (n + m) * P)

            def max_unit(k, b, g, n, beside):
                j, part_ = n // STAGES, n % STAGES
                h, u = g * HG[k] + j, g * STAGES * HG[k] + n
                if u >= 2:
                    pe.wait_ge(max_done[k], b * UNITS[k] + u - 1)
                elif k == "A" and beside:
                    pe.wait_ge(max_done["F"], UNITS["F"])
                dst = ps_max[u % 2]
                if part_ == 0:
                    last = score(k, dst[:], h, (Q[k], tile(3)), (KK[k], slice(0, S)))
                elif part_ == 1:
                    score(k, dst[:, 0:256], h, (Q[k], tile(1)), (KK[k], tile(0, 2)))
                    n0 = P if k == "A" else 2 * P
                    last = score(k, dst[:, 256:256 + n0], h, (Q[k], tile(0)), (KK[k], slice(0, n0)))
                else:
                    last = score(k, dst[:, 0:384], h, (Q[k], tile(2)), (KK[k], tile(0, 3)))
                last.then_inc(max_ready[k], 1)

            def maxima_transposed(banks, k, b, g):
                dst = free(banks, k, "T", g, (t_done[k], b * GROUPS + g + 1))
                pe.wait_ge(neg_ready[k], b * GROUPS + g + 1)
                if k == "A":
                    nc.tensor.transpose(dst[:].bitcast(BF16)[0:48, 0:P], nm_a[:, g % 2, :], ident_b[:]
                                        ).then_inc(t_ready[k], 1)
                else:
                    nc.tensor.transpose(dst[0:16, 0:P], nm_f[:, g % 2, :], ident_sb[:]).then_inc(t_ready[k], 1)

            def score_unit(k, b, g, s, j, beside):
                u, h = (g * STAGES + s) * HG[k] + j, g * HG[k] + j
                if u >= 2:
                    pe.wait_ge(exp_done[k], b * UNITS[k] + u - 1)
                elif k == "A" and beside:
                    pe.wait_ge(exp_done["F"], UNITS["F"])
                dst = ps_exp[u % 2]
                if s == 0:
                    last = score(k, dst[:], h, (KK[k], tile(0)), (Q[k], slice(0, S)))
                elif s == 1:
                    last = score(k, dst[:, 0:384], h, (KK[k], tile(1)), (Q[k], tile(1, 3)))
                else:
                    score(k, dst[:, 256:512], h, (KK[k], tile(2)), (Q[k], tile(2, 2)))
                    n0 = P if k == "A" else 2 * P
                    last = score(k, dst[:, 256 - n0:256], h, (KK[k], tile(3)), (Q[k], slice(S - n0, S)))
                last.then_inc(s_ready[k], 1)

            def weigh(k, b, n, beside):
                g, s, w = n // STAGES, n % STAGES, DV[k]
                pe.wait_ge(causal[k], b * NST + n + 1)
                if s == 0:
                    if g > 0:
                        pe.wait_ge(o_done[k], b * GROUPS + g)
                    elif k == "A" and beside:
                        pe.wait_ge(o_done["F"], GROUPS)
                        pe.wait_ge(acc_copied, 1)
                blocks = {0: [(0, 0, 0, S)], 1: [(1, 1, 0, 384)], 2: [(2, 2, P, 384), (3, 3, 0, P)]}[s]
                for dst, sums in ((ps_o, False), (ps_d, True)):
                    for kt, qt, c0, c1 in blocks:
                        for j in range(HG[k]):
                            h = g * HG[k] + j
                            left = ones[:, 0:w] if sums else val[:, kt, h * w:h * w + w]
                            last = mm(dst[j * w:j * w + w, qt * P:S], left,
                                      pt[:, (n % 2) * 4 + j, c0:c1], start=kt == 0, stop=kt == 3)
                last.then_inc(pv_done[k], 1)

            def attention(banks, k, b, beside):
                n_units = STAGES * HG[k]
                pe.wait_ge(restacked[k], (b + 1) * (16 * RESTACK[k]))
                if k == "F":
                    for sent in pair_sent:
                        pe.wait_ge(sent, 2 * 16 * 12)
                for n in range(n_units):
                    max_unit(k, b, 0, n, beside)
                for n in range(n_units):
                    max_unit(k, b, 1, n, beside)
                    if n == n_units // 2 - 1:
                        maxima_transposed(banks, k, b, 0)
                for g in range(GROUPS):
                    if g + 1 < GROUPS:
                        maxima_transposed(banks, k, b, g + 1)
                    at_sem = 16 * MROWS[k]
                    pe.wait_ge(mrow[k][g % 2], b * (2 * at_sem) + at_sem * (g // 2 + 1))
                    for s in range(STAGES):
                        for j in range(HG[k]):
                            score_unit(k, b, g, s, j, beside)
                            if g + 2 < GROUPS:
                                max_unit(k, b, g + 2, s * HG[k] + j, beside)
                        if g * STAGES + s > 0:
                            if g == 0 and s == 1:
                                wait_values(k, b)
                            weigh(k, b, g * STAGES + s - 1, beside)
                weigh(k, b, NST - 1, beside)

            def wait_values(k, b):
                if k == "A":
                    pe.wait_ge(va, (b + 1) * T)
                else:
                    pe.wait_ge(vf, (b + 1) * T)

            def expert_outputs(banks, f):
                def product(u):
                    pe.wait_ge(at_done, f * (T * E) + u + 1)
                    mm(ps_o[:], oe_sb[:, u], at[:, u % 2], start=u == 0, stop=u == T * E - 1).then_inc(at_used, 1)

                pe.wait_ge(gmt_done, f + 1)
                pe.wait_ge(o_done["F"], (f + 1) * GROUPS)
                for u in range(T * E):
                    dst = free(banks, "F", "moe2", u, (at_done, f * (T * E) + u + 1))
                    mm(dst[:], spread[:, u], gmt[:], start=True, stop=True).then_inc(sp_ready, 1)
                    if u >= 1:
                        product(u - 1)
                product(T * E - 1)

            def output(banks, f):
                dst = free(banks, "F", "out", 0, (y_done, f + 1))
                pe.wait_ge(acc_copied, f + 1)
                for t in range(T):
                    last = nc.tensor.transpose(dst[:, t * P:t * P + P], at[:, 0, t * P:t * P + P], ident_sb[:])
                last.then_inc(out_ready, 1)

            def project_back(banks, a):
                dst = free(banks, "A", "W", 0, (x1_done, a + 1))
                pe.wait_ge(gelu_done, a + 1)
                for t in range(T):
                    for g in range(GROUPS):
                        last = mm(dst[:, t * P:t * P + P], osb[:, g, t * P:t * P + P], wf_sb[:, g],
                                  start=g == 0, stop=g == GROUPS - 1)
                last.then_inc(w_ready, 1)

            pe.wait_ge(split_hi, 6)
            pe.wait_ge(split_lo, 6)
            pe.wait_ge(w_in[1], 64)
            pe.wait_ge(w_in[2], 32)
            pe.wait_ge(set_v, 8)
            pe.wait_ge(set_p, 2)

            def first(a, beside=False):
                banks = [None, None]
                project_a(banks, a)
                attention(banks, "A", 0, beside)
                project_back(banks, a)

            def experts(banks, f):
                project_f(banks, f)
                expert_values(banks, f)
                gates_transposed(banks, f)
                attention(banks, "F", 0, True)

            def body(i, f=0, a=0, beside=True):
                banks = [None, None]
                experts(banks, f)
                project_a(banks, a)
                expert_outputs(banks, f)
                output(banks, f)
                attention(banks, "A", 0, beside)
                project_back(banks, a)

            def last(i, f=0):
                banks = [None, None]
                experts(banks, f)
                expert_outputs(banks, f)
                output(banks, f)
            each_batch("pe", pe, first, body, last)

        @block.scalar
        def _(act):
            copy = lambda dst, src: nc.scalar.activation(dst, src, ACT.Copy)
            act.wait_ge(w_in[0], 16 * 8)
            for dst, c0, c1 in ((wk_h, 0, 128), (wv_h, 128, 640), (wq_h, 640, 1152), (wkf_h, 1152, 1664),
                                (wg_h, 1664, 1728)):
                copy(dst[:], gflat[:, c0:c1]).then_inc(split_hi, 1)
            act.wait_ge(w_in[2], 32)
            copy(ve_h[:], pt[:]).then_inc(split_hi, 1)

            def x_high(k, b):
                act.wait_ge(xt_ready[k], b + 1)
                copy(xh[:], ps_m[BANK[(k, "xT", 0)]][:]).then_inc(xh_done[k], 1)

            def parts_a(a, beside):
                act.wait_ge(xt_ready["A"], a + 1)
                if beside:
                    act.wait_ge(pv_done["F"], NST)
                else:
                    act.wait_ge(split_lo, 6)
                copy(part(0), ps_m[BANK[("A", "xT", 0)]][:]).then_inc(q1, 1)
                x_high("A", a)
                act.wait_ge(q_r, a + 1)
                copy(part(1), pt[:, 4]).then_inc(q2, 1)
                act.wait_ge(k_ready, a + 1)
                nc.scalar.activation(pt[:, 5], ps_m[BANK[("A", "K", 0)]][:], ACT.Identity,
                                     bias=bk_sb[:, 0:1]).then_inc(kf, 1)
                act.wait_ge(kf, a + 1)
                copy(part(3), pt[:, 5]).then_inc(k1, 1)
                act.wait_ge(k_r, a + 1)
                copy(part(4), pt[:, 6]).then_inc(k2, 1)

            def maxima(k, b, g):
                act.wait_ge(t_ready[k], b * GROUPS + g + 1)
                src = ps_m[BANK[(k, "T", g)]]
                if g >= 2:
                    n = 16 * MROWS[k]
                    act.wait_ge(mrow[k][g % 2], b * (2 * n) + n)
                if k == "A":
                    copy(mt_a[:, g % 2, :], src[:].bitcast(BF16)[0:48, 0:P]).then_inc(t_done[k], 1)
                else:
                    copy(mt_f[:, g % 2, :], src[0:16, 0:P]).then_inc(t_done[k], 1)

            def attention(k, b):
                maxima(k, b, 0)
                for g in range(GROUPS):
                    if g + 1 < GROUPS:
                        maxima(k, b, g + 1)
                    for s in range(STAGES):
                        n = g * STAGES + s
                        if n >= 2:
                            act.wait_ge(pv_done[k], b * NST + n - 1)
                        for j in range(HG[k]):
                            u = n * HG[k] + j
                            act.wait_ge(s_ready[k], b * UNITS[k] + u + 1)
                            c0, c1 = ((0, S), (0, 384), (P, S))[s]
                            nc.scalar.activation(pt[:, (n % 2) * 4 + j, 0:c1 - c0], ps_exp[u % 2][:, c0:c1],
                                                 ACT.Exp).then_inc(exp_done[k], 1)

            def gelu(a):
                act.wait_ge(o_done["A"], (a + 1) * GROUPS)
                nc.scalar.activation(osb[:], osb[:], ACT.Gelu).then_inc(gelu_done, 1)

            def experts(f):
                x_high("F", f)
                act.wait_ge(gate_ready, f + 1)
                nc.scalar.activation(g_s, ps_m[BANK[("F", "gate", 0)]][:, 0:256], ACT.Exp, scale=-1.0
                                     ).then_inc(gate_exp, 1)
                for u in range(8):
                    act.wait_ge(qk_ready, f * 8 + u + 1)
                    if u % 2 == 0 and u >= 4:
                        act.wait_ge(pair_sent[u // 2 % 2], 16 * 12)
                    nc.scalar.activation(pt[:, 4 * (u // 2 % 2) + 2 * (u % 2)].bitcast(F32R),
                                         ps_m[BANK[("F", "qk", u)]][:], ACT.Copy,
                                         scale=(SCALE, 1.0)[u % 2]).then_inc(qk_hi, 1)
                act.wait_ge(gt_made, f + 1)
                copy(gmt[:], ps_m[BANK[("F", "gmT", 0)]][:]).then_inc(gmt_done, 1)
                attention("F", f)

            def output(f):
                act.wait_ge(at_used, (f + 1) * (T * E))
                copy(at[:, 0], ps_o[:]).then_inc(acc_copied, 1)

            def first(a, beside=False):
                parts_a(a, beside)
                attention("A", a)
                gelu(a)

            def body(i, f=0, a=0, beside=True):
                experts(f)
                act.wait_ge(chosen, (f + 1) * (T * E))
                parts_a(a, beside)
                output(f)
                attention("A", a)
                gelu(a)

            def last(i, f=0):
                experts(f)
                output(f)
            each_batch("act", act, first, body, last)

        @block.gpsimd
        def _(pool):
            tt = nc.gpsimd.tensor_tensor
            nc.gpsimd.memset(half[:], -0.5).then_inc(set_p, 1)
            pool.wait_ge(set_v, 6)
            pool.wait_ge(set_p, 1)
            nc.gpsimd.affine_select(out=mask[:, S - P:S], in_=mask[:, S - P:S], compare_op=ALU.is_ge, fill=NEG,
                                    base=0, pattern=[[-1, P]], channel_multiplier=1).then_inc(set_p, 1)

            def inverse_deviation(k, b):
                pool.wait_ge(ln_ve[k], b + 1)
                tt(rstd[:], veps[:], half[:], ALU.pow).then_inc(ln_rs[k], 1)

            def residual(a):
                pool.wait_ge(ln_xn["A"], (a + 1) * T)
                tt(x_sb[:], x_sb[:], xn["A"][:], ALU.add).then_inc(resid, 1)
                pool.wait_ge(resid, 2 * a + 1)
                tt(x_sb[:], x_sb[:], bf_sb[:].unsqueeze(1).to_broadcast([P, T, D]), ALU.add).then_inc(resid, 1)

            def attention(k, b):
                for n in range(NST):
                    pool.wait_ge(exp_done[k], b * UNITS[k] + (n + 1) * HG[k])
                    s0, m = (n % 2) * 4, 2 if n % STAGES == 2 else 1
                    v = pt[:, s0:s0 + HG[k], 0:m * P].rearrange("p h (m c) -> p h m c", c=P)
                    nc.gpsimd.affine_select(out=v, in_=v, compare_op=ALU.is_ge, fill=0.0, base=0,
                                            pattern=[[0, HG[k]], [0, m], [1, P]], channel_multiplier=-1
                                            ).then_inc(causal[k], 1)

            def gated_values(f):
                for t in range(T):
                    pool.wait_ge(chosen, f * (T * E) + (t + 1) * E)
                    v = val[:, t].rearrange("p (h k) -> p h k", k=64)
                    tt(v, v, gmax[:, t * 8:t * 8 + 8].unsqueeze(2).to_broadcast([P, 8, 64]), ALU.mult
                       ).then_inc(vf, 1)

            def first(a, beside=False):
                pool.wait_ge(w_in[1], 64)
                inverse_deviation("A", a)
                residual(a)
                attention("A", a)

            def experts(f):
                inverse_deviation("F", f)
                gated_values(f)

            def body(i, f=0, a=0, beside=True):
                experts(f)
                inverse_deviation("A", a)
                residual(a)
                attention("F", f)
                attention("A", a)

            def last(i, f=0):
                experts(f)
                attention("F", f)
            each_batch("pool", pool, first, body, last)

        @block.vector
        def _(dve):
            v = nc.vector
            v.memset(s2q[:].bitcast(F32), 0.0).then_inc(set_v, 1)
            v.memset(s2k[:].bitcast(F32), 0.0).then_inc(set_v, 1)
            v.memset(s1q[:].bitcast(F32), 0.0).then_inc(set_v, 1)
            v.memset(ones[:], 1.0).then_inc(set_v, 1)
            v.memset(nm_f[:], 0.0).then_inc(set_v, 1)
            v.memset(mask[:], 0.0).then_inc(set_v, 1)
            for e in range(E):
                last = v.memset(rank[:, e:e + 1], float(E - e))
            dve.wait_ge(w_in[0], 16 * 8)
            v.tensor_copy(ident_b[:], ident_sb[:]).then_inc(set_v, 1)
            v.tensor_copy(spread[:].rearrange("r (p e) (a k) -> r p a e k", e=E, a=2)[:, 0], 
                          ident2[:, 0:16].rearrange("r (a e) -> r a e", a=2).unsqueeze(3).to_broadcast([P, 2, E, 64]))
            for p in range(1, 4):
                last = v.tensor_copy(spread[:].rearrange("r (p e) (a k) -> r p a e k", e=E, a=2)[:, p],
                                     ident2[:, 16 * p:16 * p + 16].rearrange("r (a e) -> r a e", a=2).unsqueeze(3)
                                     .to_broadcast([P, 2, E, 64]))
            last.then_inc(set_v, 1)
            for n, (hi, lo, c0, c1) in enumerate(((wk_h, wk_l, 0, 128), (wv_h, wv_l, 128, 640),
                                                  (wq_h, wq_l, 640, 1152), (wkf_h, wkf_l, 1152, 1664),
                                                  (wg_h, wg_l, 1664, 1728))):
                dve.wait_ge(split_hi, n + 1)
                v.tensor_tensor(lo[:], gflat[:, c0:c1], hi[:].bitcast(F32), ALU.subtract).then_inc(split_lo, 1)
            dve.wait_ge(split_hi, 6)
            v.tensor_tensor(ve_l[:], pt[:], ve_h[:].bitcast(F32), ALU.subtract).then_inc(split_lo, 1)

            def normalise(k, b, src):
                for t in range(T):
                    v.bn_stats(st[:, t, :], src[:, t, :]).then_inc(ln_st[k], 1)
                for t in range(T):
                    dve.wait_ge(ln_st[k], b * T + t + 1)
                    v.bn_aggr(mv[:, t, :], st[:, t, :]).then_inc(ln_mv[k], 1)
                dve.wait_ge(ln_mv[k], (b + 1) * T)
                v.tensor_scalar(veps[:], mv[:, :, 1], EPS, None, ALU.add).then_inc(ln_ve[k], 1)
                dve.wait_ge(ln_rs[k], b + 1)
                for t in range(T):
                    v.tensor_scalar(xn[k][:, t, :], src[:, t, :], mv[:, t, 0:1], rstd[:, t:t + 1],
                                    ALU.subtract, ALU.mult).then_inc(ln_xn[k], 1)

            def x_low(k, b):
                dve.wait_ge(xh_done[k], b + 1)
                v.tensor_tensor(xl[:], ps_m[BANK[(k, "xT", 0)]][:], xh[:].bitcast(F32), ALU.subtract
                                ).then_inc(xl_done[k], 1)

            def parts_a(a):
                dve.wait_ge(q1, a + 1)
                dve.wait_ge(xh_done["A"], a + 1)
                v.tensor_tensor(pt[:, 4], ps_m[BANK[("A", "xT", 0)]][:], part(0), ALU.subtract).then_inc(q_r, 1)
                x_low("A", a)
                dve.wait_ge(q2, a + 1)
                v.tensor_tensor(part(2), pt[:, 4], part(1), ALU.subtract).then_inc(q3, 1)
                dve.wait_ge(k1, a + 1)
                v.tensor_tensor(pt[:, 6], pt[:, 5], part(3), ALU.subtract).then_inc(k_r, 1)
                dve.wait_ge(k2, a + 1)
                v.tensor_tensor(part(5), pt[:, 6], part(4), ALU.subtract).then_inc(k3, 1)
                for t in range(T):
                    dve.wait_ge(v_ready, a * T + t + 1)
                    v.tensor_tensor(val[:, t], ps_m[BANK[("A", "V", t)]][:], bv_sb[:], ALU.add).then_inc(va, 1)

            def max_unit(k, b, g, n, beside):
                j, part_ = n // STAGES, n % STAGES
                u = g * STAGES * HG[k] + n
                if u >= 2:
                    dve.wait_ge(max_done[k], u - 1)
                elif k == "A" and beside:
                    dve.wait_ge(max_done["F"], UNITS["F"])
                dve.wait_ge(max_ready[k], b * UNITS[k] + u + 1)
                src = ps_max[u % 2]
                for t, c0 in (((3, 0),), ((1, 0), (0, 256)), ((2, 0),))[part_]:
                    w = (t + 1) * P
                    last = v.tensor_tensor_reduce(out=junk[:, u % 2, c0:c0 + w], in0=src[:, c0:c0 + w], in1=mask[:, S - w:S],
                                                  scale=1.0, scalar=NEG, op0=ALU.add, op1=ALU.max,
                                                  accum_out=mx[:, g % 2, 4 * j + t:4 * j + t + 1])
                last.then_inc(max_done[k], 1)

            def negate(k, b, g):
                u = (g + 1) * STAGES * HG[k]
                c = 4 * HG[k]
                m, r = mx[:, g % 2, 0:c], nm_r[:, g % 2, 0:c]
                dve.wait_ge(max_done[k], b * UNITS[k] + u)
                if g >= 2:
                    dve.wait_ge(t_ready[k], b * GROUPS + g - 1)
                if k == "A":
                    a = [nm_a[:, g % 2, 16 * n:16 * n + 16] for n in range(PARTS)]
                    at3 = b * (3 * GROUPS) + 3 * g
                    v.tensor_scalar(a[0], m, -1.0, None, ALU.mult).then_inc(neg_step[k], 1)
                    dve.wait_ge(neg_step[k], at3 + 1)
                    v.scalar_tensor_tensor(out=r, in0=m, scalar=-1.0, in1=a[0], op0=ALU.mult, op1=ALU.subtract
                                           ).then_inc(neg_step[k], 1)
                    dve.wait_ge(neg_step[k], at3 + 2)
                    v.tensor_copy(a[1], r).then_inc(neg_step[k], 1)
                    dve.wait_ge(neg_step[k], at3 + 3)
                    v.tensor_tensor(a[2], r, a[1], ALU.subtract).then_inc(neg_ready[k], 1)
                else:
                    a = [nm_f[:, g % 2, 8 * n:8 * n + 8] for n in range(2)]
                    v.tensor_scalar(a[0].bitcast(F32R), m, -1.0, None, ALU.mult).then_inc(neg_step[k], 1)
                    dve.wait_ge(neg_step[k], b * GROUPS + g + 1)
                    v.scalar_tensor_tensor(out=a[1].bitcast(F32R), in0=m, scalar=-1.0, in1=a[0], op0=ALU.mult,
                                           op1=ALU.subtract).then_inc(neg_ready[k], 1)

            def divide(k, b, g):
                dve.wait_ge(pv_done[k], b * NST + (g + 1) * STAGES)
                v.reciprocal(at[:, 1], ps_d[:]).then_inc(recip[k], 1)
                dve.wait_ge(recip[k], b * GROUPS + g + 1)
                v.tensor_tensor(osb[:, g], ps_o[:], at[:, 1], ALU.mult).then_inc(o_done[k], 1)

            def attention(k, b, beside):
                n_units = STAGES * HG[k]
                for g in range(2):
                    for n in range(n_units):
                        max_unit(k, b, g, n, beside)
                    negate(k, b, g)
                for g in range(GROUPS):
                    for s in range(STAGES):
                        if g + 2 < GROUPS:
                            for j in range(HG[k]):
                                max_unit(k, b, g + 2, s * HG[k] + j, beside)
                        if s == 0 and g > 0:
                            divide(k, b, g - 1)
                    if g + 2 < GROUPS:
                        negate(k, b, g + 2)
                divide(k, b, GROUPS - 1)

            def gate_ops(f):
                def step(n, ins):
                    ins.then_inc(gate_step, 1)

                def after(n):
                    dve.wait_ge(gate_step, f * GS + n)
                dve.wait_ge(gate_exp, f + 1)
                step(1, v.tensor_scalar(g_w, g_s, 1.0, None, ALU.add))
                yield
                after(1)
                step(2, v.reciprocal(g_s, g_w))
                yield
                after(2)
                step(3, v.tensor_reduce(gmax[:], by_head(g_s), AX.X, ALU.max))
                yield
                after(3)
                step(4, v.tensor_tensor(by_head(g_w), by_head(g_s), gmax[:].unsqueeze(2).to_broadcast([P, T * 8, E]),
                                        ALU.is_ge))
                yield
                after(4)
                step(5, v.tensor_tensor(by_head(g_w), by_head(g_w), rank[:].unsqueeze(1).to_broadcast([P, T * 8, E]),
                                        ALU.mult))
                yield
                after(5)
                step(6, v.tensor_reduce(wmax[:], by_head(g_w), AX.X, ALU.max))
                yield
                after(6)
                step(7, v.tensor_tensor(by_head(hot), by_head(g_w), wmax[:].unsqueeze(2).to_broadcast([P, T * 8, E]),
                                        ALU.is_equal))
                yield
                after(7)
                step(8, v.tensor_tensor(g_m, g_s, hot, ALU.mult))
                yield

            def gates_halves(f):
                dve.wait_ge(gate_step, (f + 1) * GS)
                gm = g_m.rearrange("p (t c) -> p t c", c=64)
                v.tensor_copy(g_t[:, :, 0:64].bitcast(F32R), gm).then_inc(gt_half, 1)
                dve.wait_ge(gt_half, f + 1)
                v.tensor_tensor(g_t[:, :, 64:128].bitcast(F32R), gm, g_t[:, :, 0:64], ALU.subtract
                                ).then_inc(gt_ready, 1)

            def experts(f):
                normalise("F", f, x1)
                x_low("F", f)
                gates = gate_ops(f)
                for u in range(8):
                    dve.wait_ge(qk_hi, f * 8 + u + 1)
                    hi = pt[:, 4 * (u // 2 % 2) + 2 * (u % 2)]
                    lo = pt[:, 4 * (u // 2 % 2) + 2 * (u % 2) + 1]
                    v.scalar_tensor_tensor(out=lo.bitcast(F32R), in0=ps_m[BANK[("F", "qk", u)]][:],
                                           scalar=(SCALE, 1.0)[u % 2], in1=hi, op0=ALU.mult, op1=ALU.subtract
                                           ).then_inc(qk_lo, 1)
                    next(gates)
                gates_halves(f)
                for t in range(T):
                    for e in range(E):
                        n = t * E + e
                        dve.wait_ge(moe1_ready, f * (T * E) + n + 1)
                        src = ps_m[BANK[("F", "moe1", n)]]
                        if e == 0:
                            v.tensor_copy(val[:, t], src[:]).then_inc(chosen, 1)
                        else:
                            dve.wait_ge(chosen, f * (T * E) + n)
                            pick = by_head(hot[:, t * 64:t * 64 + 64])[:, :, e:e + 1].to_broadcast([P, 8, 64])
                            v.copy_predicated(val[:, t].rearrange("p (h k) -> p h k", k=64), pick,
                                              src[:].rearrange("p (h k) -> p h k", k=64)).then_inc(chosen, 1)

            def expert_outputs(f):
                for u in range(T * E):
                    dve.wait_ge(sp_ready, f * (T * E) + u + 1)
                    if u >= 2:
                        dve.wait_ge(at_used, f * (T * E) + u - 1)
                    elif u == 0:
                        dve.wait_ge(o_done["F"], (f + 1) * GROUPS)
                    v.tensor_tensor(at[:, u % 2], osb[:, u // E], ps_m[BANK[("F", "moe2", u)]][:], ALU.mult
                                    ).then_inc(at_done, 1)

            def output(f):
                dve.wait_ge(out_ready, f + 1)
                v.tensor_tensor(xn["F"][:].rearrange("p t d -> p (t d)"), ps_m[BANK[("F", "out", 0)]][:],
                                x1[:].rearrange("p t d -> p (t d)"), ALU.add).then_inc(y_done, 1)

            def first_layer(a):
                dve.wait_ge(w_ready, a + 1)
                dve.wait_ge(resid, 2 * (a + 1))
                v.tensor_tensor(x1[:].rearrange("p t d -> p (t d)"), ps_m[BANK[("A", "W", 0)]][:],
                                x_sb[:].rearrange("p t d -> p (t d)"), ALU.add).then_inc(x1_done, 1)

            def first(a, beside=False):
                dve.wait_ge(x_in, 16)
                normalise("A", a, x_sb)
                parts_a(a)
                attention("A", 0, beside)
                first_layer(a)

            def body(i, f=0, a=0, beside=True):
                experts(f)
                dve.wait_ge(x_in, (a + 1) * 16)
                normalise("A", a, x_sb)
                attention("F", 0, True)
                parts_a(a)
                expert_outputs(f)
                output(f)
                attention("A", 0, beside)
                first_layer(a)

            def last(i, f=0):
                experts(f)
                attention("F", 0, True)
                expert_outputs(f)
                output(f)
            each_batch("dve", dve, first, body, last)


_NAMES = ["x", "wk", "bk", "wv", "bv", "wf", "bf", "wq", "wkf", "wg", "ve", "oe", "ident", "consts"]


def kernel(L0_attn_x, L0_attn_Wk, L0_attn_bk, L0_attn_Wv, L0_attn_bv, L0_attn_Wf, L0_attn_bf,
           L0_ffn_w_q, L0_ffn_w_k, L0_ffn_w_gate, L0_ffn_value_experts, L0_ffn_output_experts):
    import numpy as np
    import concourse.bacc as bacc
    from concourse.bass_utils import run_bass_kernel_spmd

    ve = np.transpose(np.asarray(L0_ffn_value_experts), (2, 0, 1, 3)).reshape(P, E * S)
    oe = np.asarray(L0_ffn_output_experts).reshape(E, 4, P, D).transpose(2, 1, 0, 3).reshape(P, 4 * E * D)
    wf = np.asarray(L0_attn_Wf).reshape(GROUPS, P, D).transpose(1, 0, 2).reshape(P, GROUPS * D)
    consts = np.ones((5, 4096), np.float32)
    consts[2:5] = np.full((3, 4096), 0x3F803F80, np.uint32).view(np.float32)
    values = [L0_attn_x, L0_attn_Wk, L0_attn_bk, L0_attn_Wv, L0_attn_bv, wf, L0_attn_bf, L0_ffn_w_q,
              L0_ffn_w_k, L0_ffn_w_gate, ve, oe, np.eye(P, dtype=np.float32), consts]
    nc = bacc.Bacc("TRN2", target_bir_lowering=False, num_devices=1)
    arrays, args = {}, []
    for name, a in zip(_NAMES, values):
        a = np.ascontiguousarray(a)
        arrays[f"in_{name}"] = a
        args.append(nc.dram_tensor(f"in_{name}", a.shape, mybir.dt.from_np(a.dtype), kind="ExternalInput").ap())
    out = nc.dram_tensor("out_0", (B, S, D), F32, kind="ExternalOutput").ap()
    build(nc, *args, out)
    r = run_bass_kernel_spmd(nc, [arrays], core_ids=[0])
    return r.results[0]["out_0"]
```

```python
import concourse.bass as bass
from concourse import mybir
from contextlib import ExitStack

F32 = mybir.dt.float32
F32R = mybir.dt.float32r
BF16 = mybir.dt.bfloat16
U32 = mybir.dt.uint32
ALU = mybir.AluOpType
ACT = mybir.ActivationFunctionType
AX = mybir.AxisListType

B, S, D = 8, 512, 128
P = 128
T = S // P
E = 8
HEADS = {"A": 16, "F": 8}
DV = {"A": 32, "F": 64}
GROUPS = 4
HG = {k: HEADS[k] // GROUPS for k in "AF"}
STAGES = 3
UNITS = {k: GROUPS * STAGES * HG[k] for k in "AF"}
NST = GROUPS * STAGES
DH = D // HEADS["A"]
PARTS = 3
STACK = PARTS * PARTS * DH
KROWS = 96
NEG = -3.0e38
EPS = 1e-5
SCALE = 0.125
RESTACK = {"A": 2 * PARTS + 1, "F": 2}
WRITES = 2 * PARTS
MROWS = {"A": PARTS, "F": 2}

BANK = {("F", "xT", 0): 0, ("F", "gate", 0): 1, ("F", "gmT", 0): 0, ("A", "xT", 0): 0, ("A", "K", 0): 0,
        ("F", "acc", 0): 1, ("F", "out", 0): 0, ("A", "W", 0): 1}
BANK.update({("F", "qk", u): u % 2 for u in range(8)})
BANK.update({("F", "moe1", u): u % 4 for u in range(T * E)})
BANK.update({("F", "moe2", u): 0 for u in range(T * E)})
BANK.update({(k, "T", g): 0 for k in "AF" for g in range(GROUPS)})
BANK.update({("A", "V", t): 2 + t % 2 for t in range(T)})


def place(counts):
    at, u = {}, 0
    for phase, per_step in counts:
        for n, c in enumerate(per_step):
            at[phase, n] = range(u, u + c)
            u += c
    assert u == T * E
    return at


OUTPUTS = place([("F", [0] * 12 + [1, 0] * 6), ("gap", [2]), ("pre", [1, 0] * 12),
                 ("A", ([1, 0, 0, 0] * 12)[:48])])


def build(nc, x, wk, bk, wv, bv, wf, bf, wq, wkf, wg, ve, oe, ident, consts, out):
    ctx = ExitStack()
    with ctx:
        def sb(name, shape, dt=F32):
            return ctx.enter_context(nc.sbuf_tensor(name, shape, dt))

        sems = []

        def sem(name):
            sems.append(ctx.enter_context(nc.semaphore(name)))
            return sems[-1]

        wk_h, wk_l = sb("wk_h", [P, D], F32R), sb("wk_l", [P, D], F32R)
        wv_h, wv_l = sb("wv_h", [P, S], F32R), sb("wv_l", [P, S], F32R)
        wq_h, wq_l = sb("wq_h", [P, S], F32R), sb("wq_l", [P, S], F32R)
        wkf_h, wkf_l = sb("wkf_h", [P, S], F32R), sb("wkf_l", [P, S], F32R)
        wg_h, wg_l = sb("wg_h", [P, 64], F32R), sb("wg_l", [P, 64], F32R)
        ve_h, ve_l = sb("ve_h", [P, E, S], F32R), sb("ve_l", [P, E, S], F32R)
        oe_sb = sb("oe_sb", [P, 4 * E, D])
        wf_sb = sb("wf_sb", [P, GROUPS, D])
        spread = sb("spread", [P, 4 * E, P], F32R)
        ident_sb = sb("ident_sb", [P, P])
        ident_b = sb("ident_b", [P, P], BF16)
        ident2 = sb("ident2", [P, 64])
        ones = sb("ones", [P, 64])
        mask = sb("mask", [P, S], BF16)
        bk_sb = sb("bk_sb", [P, 1])
        bv_sb = sb("bv_sb", [P, S])
        bf_sb = sb("bf_sb", [P, D])
        rank = sb("rank", [P, E])
        half = sb("half", [P, T])
        x_sb = sb("x_sb", [P, T, D])
        xn = {k: sb(f"xn{k}", [P, T, D]) for k in "AF"}
        x1 = sb("x1", [P, T, D])
        xh, xl = sb("xh", [P, S], F32R), sb("xl", [P, S], F32R)
        s1q, s1k = sb("s1q", [P, 8, S], F32R), sb("s1k", [P, 8, S], F32R)
        s2q, s2k = sb("s2q", [P, 8, S], F32R), sb("s2k", [P, 8, S], F32R)
        qs = s1q[:].rearrange("p a b -> p (a b)").bitcast(BF16).rearrange("p (h n) -> p h n", n=S)
        ks = s2k[:].rearrange("p a b -> p (a b)").bitcast(BF16).rearrange("p (h n) -> p h n", n=S)
        val = sb("val", [P, T, S])
        osb = sb("osb", [P, GROUPS, S])
        pt = sb("pt", [P, 8, S])
        at = sb("at", [P, 2, S])
        y_sb = at[:, 1]
        den = sb("den", [P, 2, S])
        gmt = sb("gmt", [P, S], F32R)
        junk = sb("junk", [P, 2, S], BF16)
        mx = sb("mx", [P, 2, 16])
        nm_r = sb("nm_r", [P, 2, 16])
        nm_a = sb("nm_a", [P, 2, 48], BF16)
        nm_f = sb("nm_f", [P, 2, 16])
        mt_a = sb("mt_a", [48, 2, P], BF16)
        mt_f = sb("mt_f", [16, 2, P])
        st = sb("st", [P, T, 6])
        mv = sb("mv", [P, T, 2])
        veps, rstd = sb("veps", [P, T]), sb("rstd", [P, T])
        gmax, wmax = sb("gmax", [P, T * 8]), sb("wmax", [P, T * 8])
        gflat = osb[:].rearrange("p a b -> p (a b)")
        g_s, g_w, g_m = gflat[:, 0:256], gflat[:, 256:512], gflat[:, 512:768]
        hot = gflat[:, 768:1024].bitcast(U32)
        g_t = gflat[:, 1024:1536].rearrange("p (t c) -> p t c", c=P)

        ve_raw = oe_sb[:].rearrange("p (e c) d -> p e (c d)", e=E)
        rest = pt[:, 7]

        def part(n):
            return pt[:, (2, 3, 6)[n // 2], :].bitcast(BF16)[:, (n % 2) * S:(n % 2) * S + S]

        def by_head(ap):
            return ap.rearrange("p (a e) -> p a e", e=E)

        def bank(name):
            return ctx.enter_context(nc.psum_tensor(name, [P, S], F32))
        ps_max = [bank("ps_max0"), bank("ps_max1")]
        ps_exp = [bank("ps_exp0"), bank("ps_exp1")]
        ps_o, ps_d = bank("ps_o"), bank("ps_d")
        ps_m = [bank("ps_m0"), bank("ps_m1")] + ps_exp

        parts_d = {n: nc.dram_tensor(f"parts_{n}", (PARTS, DH, HEADS["A"], S), BF16).ap() for n in "qk"}
        zeros_d = nc.dram_tensor("zeros_d", (4, 4096), F32).ap()
        ones_d = nc.dram_tensor("ones_d", (2, 4096), F32).ap()
        onesb_d = nc.dram_tensor("onesb_d", (PARTS, 8192), BF16).ap()

        w_in = [sem(f"w_in{n}") for n in range(3)]
        split_hi, split_lo = sem("split_hi"), sem("split_lo")
        oe_in = sem("oe_in")
        set_v, set_p = sem("set_v"), sem("set_p")
        cst = sem("cst")
        cleared = {n: sem(f"cleared_{n}") for n in ("sp", "pe", "act", "pool", "dve")}
        y_out = sem("y_out")
        first_of_batch = len(sems)
        arrived = sem("arrived")
        x_in = sem("x_in")
        K2 = lambda n: {k: sem(f"{n}{k}") for k in "AF"}
        ln_st, ln_mv, ln_ve, ln_rs, ln_xn = (K2(n) for n in ("ln_st", "ln_mv", "ln_ve", "ln_rs", "ln_xn"))
        xt_ready, xh_done, xl_done = K2("xt_ready"), K2("xh_done"), K2("xl_done")
        restacked = K2("restacked")
        pair_sent = [sem("pair_sent0"), sem("pair_sent1")]
        max_ready, max_done = K2("max_ready"), K2("max_done")
        neg_step, neg_ready = K2("neg_step"), K2("neg_ready")
        t_ready, t_done = K2("t_ready"), K2("t_done")
        mrow = {k: [sem(f"mrow{k}{n}") for n in range(2)] for k in "AF"}
        s_ready, exp_done = K2("s_ready"), K2("exp_done")
        causal, pv_done, recip, o_done = K2("causal"), K2("pv_done"), K2("recip"), K2("o_done")
        sums_out = K2("sums_out")
        q1, q_r, q2, q3 = sem("q1"), sem("q_r"), sem("q2"), sem("q3")
        k_ready, kf, k1, k_r, k2, k3 = (sem(n) for n in ("k_ready", "kf", "k1", "k_r", "k2", "k3"))
        parts_out = sem("parts_out")
        v_ready, va = sem("v_ready"), sem("va")
        resid = sem("resid")
        gelu_done, w_ready, x1_done = sem("gelu_done"), sem("w_ready"), sem("x1_done")
        gate_ready, gate_exp, gate_step, gt_ready, gmt_done = (
            sem(n) for n in ("gate_ready", "gate_exp", "gate_step", "gt_ready", "gmt_done"))
        gt_made, gt_half = sem("gt_made"), sem("gt_half")
        qk_ready, qk_hi, qk_lo = sem("qk_ready"), sem("qk_hi"), sem("qk_lo")
        moe1_ready, chosen, vf = sem("moe1_ready"), sem("chosen"), sem("vf")
        sp_ready, at_done, at_used = sem("sp_ready"), sem("at_done"), sem("at_used")
        acc_copied, out_ready, y_done = (sem(n) for n in ("acc_copied", "out_ready", "y_done"))

        numbers = [s.num for s in sems[first_of_batch:]]
        per_batch = range(numbers[0], numbers[-1] + 1)
        assert numbers == list(per_batch)

        block = ctx.enter_context(nc.Block())
        GS = 8

        def each_batch(name, eng, first, body, last):
            def meet():
                eng.drain().then_inc(arrived, 1)
                if name == "sp":
                    eng.wait_ge(arrived, 5)
                    eng.sem_clear(per_batch)
                    for go in cleared.values():
                        eng.sem_inc(go, 1)
                eng.wait_ge(cleared[name], 1)
                eng.sem_clear(cleared[name])
            first()
            meet()
            with eng.Fori(0, B - 1) as i:
                body(i)
                meet()
            last(B - 1)

        @block.sync
        def _(sp):
            o = gflat
            sp.dma_start(x_sb[:], x[0].rearrange("(t p) d -> p t d", p=P)).then_inc(x_in, 16)
            sp.dma_start(ident_sb[:], ident).then_inc(w_in[0], 16)
            sp.dma_start(o[:, 0:128], wk).then_inc(w_in[0], 16)
            sp.dma_start(o[:, 128:640], wv).then_inc(w_in[0], 16)
            sp.dma_start(bk_sb[:], bk.rearrange("(p o) -> p o", o=1)).then_inc(w_in[0], 16)
            sp.dma_start(zeros_d, consts[5:9]).then_inc(cst, 16)
            sp.dma_start(ones_d, consts[0:2]).then_inc(cst, 16)
            sp.dma_start(onesb_d, consts[2:5].bitcast(BF16)).then_inc(cst, 16)
            sp.wait_ge(cst, 16 * 3)
            sp.wait_ge(set_p, 3)
            sp.dma_start(ks[STACK:STACK + PARTS], onesb_d.rearrange("p (h n) -> p h n", n=S)).then_inc(cst, 16)
            sp.dma_start(bf_sb[:], bf.partition_broadcast(P)).then_inc(w_in[1], 16)
            sp.dma_start(bv_sb[:], bv.partition_broadcast(P)).then_inc(w_in[1], 16)
            sp.dma_start(wf_sb[:], wf.rearrange("p (g d) -> p g d", d=D)).then_inc(w_in[1], 16)
            sp.sem_inc(y_out, 16)

            def parts_to_dram(name):
                first_part, ready = {"q": (0, (q1, q2, q3)), "k": (PARTS, (k1, k2, k3))}[name]
                for m in range(PARTS):
                    sp.wait_ge(ready[m], 1)
                    sp.dma_start(parts_d[name][m].rearrange("d h n -> h d n"), part(first_part + m)
                                 ).then_inc(parts_out, 16)

            def restack_a():
                sp.wait_ge(parts_out, 16 * WRITES)
                n_rows = PARTS * DH
                for m in range(PARTS):
                    sp.dma_start(ks[m * n_rows:(m + 1) * n_rows], parts_d["k"].rearrange("m d h n -> (m d) h n")
                                 ).then_inc(restacked["A"], 16)
                    sp.dma_start(qs[m * n_rows:(m + 1) * n_rows],
                                 parts_d["q"][m:m + 1].to_broadcast([PARTS, DH, HEADS["A"], S])
                                 ).then_inc(restacked["A"], 16)
                sp.dma_start(qs[STACK:STACK + PARTS],
                             zeros_d[0:3].bitcast(BF16).rearrange("p (h n) -> p h n", n=S)
                             ).then_inc(restacked["A"], 16)

            def restack_f():
                sp.dma_start(s2q[64:66].bitcast(F32), zeros_d[0:2].rearrange("p (h n) -> p h n", n=S)
                             ).then_inc(restacked["F"], 16)
                sp.dma_start(s2k[64:66].bitcast(F32), ones_d.rearrange("p (h n) -> p h n", n=S)
                             ).then_inc(restacked["F"], 16)
                for p in range(4):
                    sp.wait_ge(qk_lo, 2 * p + 2)
                    qh, ql, kh, kl = (pt[:, 4 * (p % 2) + n, :] for n in range(4))
                    for ab in range(2):
                        r, h = slice(64 * ab, 64 * ab + 64), 2 * p + ab
                        for dst, src in ((s1q[0:64, h], qh), (s1q[64:128, h], ql), (s1k[0:64, h], kh),
                                         (s1k[64:128, h], kh), (s2q[0:64, h], qh), (s2k[0:64, h], kl)):
                            sp.dma_start(dst.bitcast(F32), src[r]).then_inc(pair_sent[p % 2], 16)

            def maxima_rows(k, g):
                sp.wait_ge(t_done[k], g + 1)
                for m in range(MROWS[k]):
                    if k == "A":
                        dst, src = qs[STACK + m:STACK + m + 1, 4 * g:4 * g + 4], mt_a[16 * m:16 * m + 16, g % 2]
                    else:
                        dst = s2q[64 + m:65 + m, 2 * g:2 * g + 2].bitcast(F32)
                        src = mt_f[8 * m:8 * m + 8, g % 2]
                    sp.dma_start(dst.rearrange("o h (t n) -> o (h t) n", n=P), src).then_inc(mrow[k][g % 2], 16)

            def attention_a():
                for g in range(GROUPS):
                    maxima_rows("A", g)

            def attention_f(next_batch):
                for g in range(GROUPS):
                    if next_batch and g >= 2:
                        parts_to_dram({2: "q", 3: "k"}[g])
                    maxima_rows("F", g)

            def store(i):
                sp.wait_ge(y_done, 1)
                dst = out[i] if isinstance(i, int) else out[bass.ds(i, 1)].rearrange("o s d -> (o s) d")
                sp.dma_start(dst.rearrange("(t p) d -> p t d", p=P), y_sb.rearrange("p (t d) -> p t d", d=D)).then_inc(y_out, 16)

            def store_landed():
                sp.wait_ge(y_out, 16)
                sp.sem_clear(y_out)

            def first():
                parts_to_dram("q")
                parts_to_dram("k")
                restack_a()
                for dst, src in ((o[:, 640:1152], wq), (o[:, 1152:1664], wkf), (o[:, 1664:1728], wg),
                                 (ident2[0:64, :], ident[0:64, 0:64]), (ident2[64:128, :], ident[0:64, 0:64]),
                                 (ve_raw, ve.rearrange("p (e n) -> p e n", n=S))):
                    sp.dma_start(dst, src).then_inc(w_in[2], 16)
                sp.wait_ge(split_hi, 6)
                sp.wait_ge(split_lo, 6)
                sp.dma_start(oe_sb[:], oe.rearrange("p (c d) -> p c d", d=D)).then_inc(oe_in, 16)
                attention_a()

            def body(i):
                sp.dma_start(x_sb[:], x[bass.ds(i + 1, 1)].rearrange("o (t p) d -> p (o t) d", p=P)).then_inc(x_in, 16)
                restack_f()
                store_landed()
                attention_f(True)
                sp.wait_ge(s_ready["F"], UNITS["F"])
                restack_a()
                attention_a()
                store(i)

            def last(i):
                restack_f()
                store_landed()
                attention_f(False)
                store(i)
                sp.wait_ge(y_out, 16)
            each_batch("sp", sp, first, body, last)

        @block.tensor
        def _(pe):
            mm = nc.tensor.matmul

            def mm3(dst, lh, ll, rh, rl):
                mm(dst, lh, rh, start=True, stop=False)
                mm(dst, ll, rh, start=False, stop=False)
                return mm(dst, lh, rl, start=False, stop=True)

            def free(banks, k, name, n, drained):
                b = BANK[(k, name, n)]
                if banks[b] is not None:
                    pe.wait_ge(*banks[b])
                banks[b] = drained
                return ps_m[b]

            def transposed(banks, k):
                dst = free(banks, k, "xT", 0, (xl_done[k], 1))
                pe.wait_ge(ln_xn[k], T)
                for t in range(T):
                    last = nc.tensor.transpose(dst[:, t * P:t * P + P], xn[k][:, t, :], ident_sb[:])
                last.then_inc(xt_ready[k], 1)

            def keys_a(banks):
                pe.wait_ge(xl_done["A"], 1)
                dst = free(banks, "A", "K", 0, (kf, 1))
                mm3(dst[:], wk_h[:], wk_l[:], xh[:], xl[:]).then_inc(k_ready, 1)

            def values_a(banks, beside):
                if beside:
                    pe.wait_ge(exp_done["F"], UNITS["F"])
                for t in range(T):
                    dst = free(banks, "A", "V", t, (va, t + 1))
                    r = slice(t * P, t * P + P)
                    mm3(dst[:], xh[:, r], xl[:, r], wv_h[:], wv_l[:]).then_inc(v_ready, 1)

            def project_f(banks):
                transposed(banks, "F")
                pe.wait_ge(xl_done["F"], 1)
                dst = free(banks, "F", "gate", 0, (gate_exp, 1))
                for t in range(T):
                    r = slice(t * P, t * P + P)
                    last = mm3(dst[:, t * 64:t * 64 + 64], xh[:, r], xl[:, r], wg_h[:], wg_l[:])
                last.then_inc(gate_ready, 1)
                for u in range(8):
                    wh, wl = ((wq_h, wq_l), (wkf_h, wkf_l))[u % 2]
                    c = slice(u // 2 * P, u // 2 * P + P)
                    dst = free(banks, "F", "qk", u, (qk_lo, u + 1))
                    mm3(dst[:], wh[:, c], wl[:, c], xh[:], xl[:]).then_inc(qk_ready, 1)

            def expert_values(banks):
                for t in range(T):
                    r = slice(t * P, t * P + P)
                    for e in range(E):
                        dst = free(banks, "F", "moe1", t * E + e, (chosen, t * E + e + 1))
                        mm3(dst[:], xh[:, r], xl[:, r], ve_h[:, e], ve_l[:, e]).then_inc(moe1_ready, 1)

            def gates_transposed(banks):
                dst = free(banks, "F", "gmT", 0, (gmt_done, 1))
                pe.wait_ge(gt_ready, 1)
                for t in range(T):
                    last = nc.tensor.transpose(dst[:, t * P:t * P + P], g_t[:, t, :], ident_sb[:])
                last.then_inc(gt_made, 1)

            def score(k, dst, h, rows, cols):
                (l1, l2), (r1, r2) = rows, cols
                if k == "A":
                    return mm(dst, l1[0:KROWS, h, l2], r1[0:KROWS, h, r2], start=True, stop=True)
                mm(dst, l1[0][:, h, l2], r1[0][:, h, r2], start=True, stop=False)
                return mm(dst, l1[1][0:KROWS, h, l2], r1[1][0:KROWS, h, r2], start=False, stop=True)

            Q = {"A": qs, "F": (s1q, s2q)}
            KK = {"A": ks, "F": (s1k, s2k)}

            def tile(n, m=1):
                return slice(n * P, (n + m) * P)

            def max_unit(k, g, n, beside):
                j, part_ = n // STAGES, n % STAGES
                h, u = g * HG[k] + j, g * STAGES * HG[k] + n
                if u >= 2:
                    pe.wait_ge(max_done[k], u - 1)
                elif k == "A" and beside:
                    pe.wait_ge(max_done["F"], UNITS["F"])
                dst = ps_max[u % 2]
                if part_ == 0:
                    last = score(k, dst[:], h, (Q[k], tile(3)), (KK[k], slice(0, S)))
                elif part_ == 1:
                    score(k, dst[:, 0:256], h, (Q[k], tile(1)), (KK[k], tile(0, 2)))
                    n0 = P if k == "A" else 2 * P
                    last = score(k, dst[:, 256:256 + n0], h, (Q[k], tile(0)), (KK[k], slice(0, n0)))
                else:
                    last = score(k, dst[:, 0:384], h, (Q[k], tile(2)), (KK[k], tile(0, 3)))
                last.then_inc(max_ready[k], 1)

            def maxima_transposed(banks, k, g):
                dst = free(banks, k, "T", g, (t_done[k], g + 1))
                pe.wait_ge(neg_ready[k], g + 1)
                if k == "A":
                    nc.tensor.transpose(dst[:].bitcast(BF16)[0:48, 0:P], nm_a[:, g % 2, :], ident_b[:]
                                        ).then_inc(t_ready[k], 1)
                else:
                    nc.tensor.transpose(dst[0:16, 0:P], nm_f[:, g % 2, :], ident_sb[:]).then_inc(t_ready[k], 1)

            def score_unit(k, g, s, j):
                u, h = (g * STAGES + s) * HG[k] + j, g * HG[k] + j
                if u >= 2:
                    pe.wait_ge(exp_done[k], u - 1)
                elif k == "A":
                    pe.wait_ge(va, T)
                else:
                    pe.wait_ge(chosen, T * E)
                dst = ps_exp[u % 2]
                if s == 0:
                    last = score(k, dst[:], h, (KK[k], tile(0)), (Q[k], slice(0, S)))
                elif s == 1:
                    last = score(k, dst[:, 0:384], h, (KK[k], tile(1)), (Q[k], tile(1, 3)))
                else:
                    score(k, dst[:, 256:512], h, (KK[k], tile(2)), (Q[k], tile(2, 2)))
                    n0 = P if k == "A" else 2 * P
                    last = score(k, dst[:, 256 - n0:256], h, (KK[k], tile(3)), (Q[k], slice(S - n0, S)))
                last.then_inc(s_ready[k], 1)

            def weigh(k, n, beside):
                g, s, w = n // STAGES, n % STAGES, DV[k]
                pe.wait_ge(causal[k], n + 1)
                if s == 0:
                    if g > 0:
                        pe.wait_ge(sums_out[k], g)
                    elif k == "A" and beside:
                        pe.wait_ge(sums_out["F"], GROUPS)
                blocks = {0: [(0, 0, 0, S)], 1: [(1, 1, 0, 384)], 2: [(2, 2, P, 384), (3, 3, 0, P)]}[s]
                for dst, sums in ((ps_d, True), (ps_o, False)):
                    for kt, qt, c0, c1 in blocks:
                        for j in range(HG[k]):
                            h = g * HG[k] + j
                            left = ones[:, 0:w] if sums else val[:, kt, h * w:h * w + w]
                            last = mm(dst[j * w:j * w + w, qt * P:S], left,
                                      pt[:, (n % 2) * 4 + j, c0:c1], start=kt == 0, stop=kt == 3)
                last.then_inc(pv_done[k], 1)

            def product(u):
                pe.wait_ge(at_done, u + 1)
                mm(ps_m[1][:], oe_sb[:, u], at[:, u % 2], start=u == 0, stop=u == T * E - 1).then_inc(at_used, 1)

            def outputs(banks, phase, n):
                for u in OUTPUTS[phase, n]:
                    if u == 0:
                        free(banks, "F", "acc", 0, (acc_copied, 1))
                        pe.wait_ge(gmt_done, 1)
                    dst = free(banks, "F", "moe2", u, (at_done, u + 1))
                    mm(dst[:], spread[:, u], gmt[:], start=True, stop=True).then_inc(sp_ready, 1)
                    if u >= 1:
                        product(u - 1)

            def outputs_end(banks):
                product(T * E - 1)
                dst = free(banks, "F", "out", 0, (y_done, 1))
                pe.wait_ge(acc_copied, 1)
                for t in range(T):
                    last = nc.tensor.transpose(dst[:, t * P:t * P + P], at[:, 0, t * P:t * P + P], ident_sb[:])
                last.then_inc(out_ready, 1)

            def attention(banks, k, beside):
                n_units = STAGES * HG[k]
                pe.wait_ge(restacked[k], 16 * RESTACK[k])
                if k == "F":
                    for sent in pair_sent:
                        pe.wait_ge(sent, 2 * 16 * 12)
                for g in range(2):
                    for n in range(n_units):
                        max_unit(k, g, n, beside)
                        if k == "A" and beside:
                            outputs(banks, "pre", g * n_units + n)
                        if g == 1 and n == n_units // 2 - 1:
                            maxima_transposed(banks, k, 0)
                if k == "F" and beside:
                    transposed(banks, "A")
                for g in range(GROUPS):
                    if g + 1 < GROUPS:
                        maxima_transposed(banks, k, g + 1)
                    pe.wait_ge(mrow[k][g % 2], 16 * MROWS[k] * (g // 2 + 1))
                    for s in range(STAGES):
                        n = g * STAGES + s
                        for j in range(HG[k]):
                            score_unit(k, g, s, j)
                            if g + 2 < GROUPS:
                                max_unit(k, g + 2, s * HG[k] + j, beside)
                            if k == "F" or beside:
                                outputs(banks, k, n * HG[k] + j)
                        if n > 0:
                            if n == 1 and k == "F":
                                pe.wait_ge(vf, T)
                            weigh(k, n - 1, beside)
                        if n == 2 and k == "F" and beside:
                            keys_a(banks)
                weigh(k, NST - 1, beside)

            def project_back(banks):
                dst = free(banks, "A", "W", 0, (x1_done, 1))
                for g in range(GROUPS):
                    if g == 0 or g == GROUPS - 1:
                        pe.wait_ge(gelu_done, 1 if g == 0 else 2)
                    for t in range(T):
                        last = mm(dst[:, t * P:t * P + P], osb[:, g, t * P:t * P + P], wf_sb[:, g],
                                  start=g == 0 and t == 0, stop=g == GROUPS - 1 and t == T - 1)
                last.then_inc(w_ready, 1)

            def first():
                banks = [None] * 4
                pe.wait_ge(w_in[0], 16 * 4)
                transposed(banks, "A")
                pe.wait_ge(split_hi, 2)
                pe.wait_ge(split_lo, 2)
                keys_a(banks)
                values_a(banks, False)
                pe.wait_ge(cst, 16 * 4)
                pe.wait_ge(set_v, 5)
                pe.wait_ge(set_p, 4)
                attention(banks, "A", False)
                pe.wait_ge(w_in[1], 16 * 3)
                project_back(banks)
                pe.wait_ge(split_hi, 6)
                pe.wait_ge(split_lo, 6)
                pe.wait_ge(w_in[2], 16 * 6)
                pe.wait_ge(oe_in, 16)

            def experts(banks, next_batch):
                project_f(banks)
                expert_values(banks)
                gates_transposed(banks)
                attention(banks, "F", next_batch)

            def body(i):
                banks = [None] * 4
                experts(banks, True)
                values_a(banks, True)
                outputs(banks, "gap", 0)
                attention(banks, "A", True)
                outputs_end(banks)
                project_back(banks)

            def last(i):
                banks = [None] * 4
                experts(banks, False)
                for phase, n in OUTPUTS:
                    if phase != "F":
                        outputs(banks, phase, n)
                outputs_end(banks)
            each_batch("pe", pe, first, body, last)

        @block.scalar
        def _(act):
            copy = lambda dst, src: nc.scalar.activation(dst, src, ACT.Copy)

            def x_high(k):
                act.wait_ge(xt_ready[k], 1)
                copy(xh[:], ps_m[BANK[(k, "xT", 0)]][:]).then_inc(xh_done[k], 1)

            def q_part0(beside):
                act.wait_ge(xt_ready["A"], 1)
                if beside:
                    for sent in pair_sent:
                        act.wait_ge(sent, 2 * 16 * 12)
                copy(part(0), ps_m[BANK[("A", "xT", 0)]][:]).then_inc(q1, 1)
                x_high("A")

            def q_part1():
                act.wait_ge(q_r, 1)
                copy(part(1), rest).then_inc(q2, 1)

            def k_part0():
                act.wait_ge(k_ready, 1)
                act.wait_ge(q3, 1)
                nc.scalar.activation(rest, ps_m[BANK[("A", "K", 0)]][:], ACT.Identity,
                                     bias=bk_sb[:, 0:1]).then_inc(kf, 1)
                act.wait_ge(kf, 1)
                copy(part(3), rest).then_inc(k1, 1)

            def k_part1():
                act.wait_ge(k_r, 1)
                copy(part(4), rest).then_inc(k2, 1)

            def maxima(k, g):
                act.wait_ge(t_ready[k], g + 1)
                src = ps_m[BANK[(k, "T", g)]]
                if g >= 2:
                    act.wait_ge(mrow[k][g % 2], 16 * MROWS[k])
                if k == "A":
                    copy(mt_a[:, g % 2, :], src[:].bitcast(BF16)[0:48, 0:P]).then_inc(t_done[k], 1)
                else:
                    copy(mt_f[:, g % 2, :], src[0:16, 0:P]).then_inc(t_done[k], 1)

            def sums(k, g, beside):
                act.wait_ge(pv_done[k], (g + 1) * STAGES)
                if g >= 2:
                    act.wait_ge(o_done[k], g - 1)
                if k == "A" and beside:
                    act.wait_ge(at_done, (g + 1) * E)
                copy(den[:, g % 2], ps_d[:])
                copy(osb[:, g], ps_o[:]).then_inc(sums_out[k], 1)

            def attention(k, beside):
                maxima(k, 0)
                if k == "F" and beside:
                    q_part0(beside)
                for g in range(GROUPS):
                    if g + 1 < GROUPS:
                        maxima(k, g + 1)
                    for s in range(STAGES):
                        n = g * STAGES + s
                        if n >= 2:
                            act.wait_ge(pv_done[k], n - 1)
                        for j in range(HG[k]):
                            u = n * HG[k] + j
                            act.wait_ge(s_ready[k], u + 1)
                            c0, c1 = ((0, S), (0, 384), (P, S))[s]
                            nc.scalar.activation(pt[:, (n % 2) * 4 + j, 0:c1 - c0], ps_exp[u % 2][:, c0:c1],
                                                 ACT.Exp).then_inc(exp_done[k], 1)
                        if s == 0 and g > 0:
                            sums(k, g - 1, beside)
                        if k == "F" and beside:
                            if n == 0:
                                q_part1()
                            elif n == 2:
                                k_part0()
                            elif n == 3:
                                k_part1()
                sums(k, GROUPS - 1, beside)

            def gelu():
                for n, groups in enumerate((slice(0, GROUPS - 1), slice(GROUPS - 1, GROUPS))):
                    act.wait_ge(o_done["A"], GROUPS - 1 + n)
                    nc.scalar.activation(osb[:, groups], osb[:, groups], ACT.Gelu).then_inc(gelu_done, 1)

            def experts(next_batch):
                x_high("F")
                act.wait_ge(gate_ready, 1)
                nc.scalar.activation(g_s, ps_m[BANK[("F", "gate", 0)]][:, 0:256], ACT.Exp, scale=-1.0
                                     ).then_inc(gate_exp, 1)
                for u in range(8):
                    act.wait_ge(qk_ready, u + 1)
                    if u % 2 == 0 and u >= 4:
                        act.wait_ge(pair_sent[u // 2 % 2], 16 * 12)
                    nc.scalar.activation(pt[:, 4 * (u // 2 % 2) + 2 * (u % 2)].bitcast(F32R),
                                         ps_m[BANK[("F", "qk", u)]][:], ACT.Copy,
                                         scale=(SCALE, 1.0)[u % 2]).then_inc(qk_hi, 1)
                act.wait_ge(gt_made, 1)
                copy(gmt[:], ps_m[BANK[("F", "gmT", 0)]][:]).then_inc(gmt_done, 1)
                attention("F", next_batch)

            def outputs_end():
                act.wait_ge(at_used, T * E)
                copy(at[:, 0], ps_m[BANK[("F", "acc", 0)]][:]).then_inc(acc_copied, 1)

            def first():
                act.wait_ge(w_in[0], 16 * 4)
                copy(wk_h[:], gflat[:, 0:128]).then_inc(split_hi, 1)
                copy(wv_h[:], gflat[:, 128:640]).then_inc(split_hi, 1)
                q_part0(False)
                q_part1()
                k_part0()
                k_part1()
                act.wait_ge(w_in[2], 16 * 6)
                for dst, c0, c1 in ((wq_h, 640, 1152), (wkf_h, 1152, 1664), (wg_h, 1664, 1728)):
                    copy(dst[:], gflat[:, c0:c1]).then_inc(split_hi, 1)
                copy(ve_h[:], ve_raw).then_inc(split_hi, 1)
                act.wait_ge(split_lo, 6)
                attention("A", False)
                gelu()

            def body(i):
                experts(True)
                attention("A", True)
                outputs_end()
                gelu()

            def last(i):
                experts(False)
                outputs_end()
            each_batch("act", act, first, body, last)

        @block.gpsimd
        def _(pool):
            tt = nc.gpsimd.tensor_tensor
            nc.gpsimd.memset(half[:], -0.5).then_inc(set_p, 1)

            def inverse_deviation(k):
                pool.wait_ge(ln_ve[k], 1)
                tt(rstd[:], veps[:], half[:], ALU.pow).then_inc(ln_rs[k], 1)

            def residual():
                pool.wait_ge(ln_xn["A"], T)
                tt(x_sb[:], x_sb[:], xn["A"][:], ALU.add).then_inc(resid, 1)
                pool.wait_ge(resid, 1)
                tt(x_sb[:], x_sb[:], bf_sb[:].unsqueeze(1).to_broadcast([P, T, D]), ALU.add).then_inc(resid, 1)

            def attention(k):
                for n in range(NST):
                    pool.wait_ge(exp_done[k], (n + 1) * HG[k])
                    s0, m = (n % 2) * 4, 2 if n % STAGES == 2 else 1
                    v = pt[:, s0:s0 + HG[k], 0:m * P].rearrange("p h (m c) -> p h m c", c=P)
                    nc.gpsimd.affine_select(out=v, in_=v, compare_op=ALU.is_ge, fill=0.0, base=0,
                                            pattern=[[0, HG[k]], [0, m], [1, P]], channel_multiplier=-1
                                            ).then_inc(causal[k], 1)

            def gated_values():
                for t in range(T):
                    pool.wait_ge(chosen, (t + 1) * E)
                    v = val[:, t].rearrange("p (h k) -> p h k", k=64)
                    tt(v, v, gmax[:, t * 8:t * 8 + 8].unsqueeze(2).to_broadcast([P, 8, 64]), ALU.mult
                       ).then_inc(vf, 1)

            def first():
                pool.wait_ge(set_p, 1)
                inverse_deviation("A")
                nc.gpsimd.memset(s2q[:].bitcast(F32), 0.0).then_inc(set_p, 1)
                nc.gpsimd.memset(s2k[:].bitcast(F32), 0.0).then_inc(set_p, 1)
                pool.wait_ge(set_v, 3)
                nc.gpsimd.affine_select(out=mask[:, S - P:S], in_=mask[:, S - P:S], compare_op=ALU.is_ge, fill=NEG,
                                        base=0, pattern=[[-1, P]], channel_multiplier=1).then_inc(set_p, 1)
                pool.wait_ge(w_in[1], 16 * 3)
                residual()
                attention("A")

            def experts():
                inverse_deviation("F")
                gated_values()

            def body(i):
                experts()
                inverse_deviation("A")
                residual()
                attention("F")
                attention("A")

            def last(i):
                experts()
                attention("F")
            each_batch("pool", pool, first, body, last)

        @block.vector
        def _(dve):
            v = nc.vector

            def normalise(k, src):
                for t in range(T):
                    v.bn_stats(st[:, t, :], src[:, t, :]).then_inc(ln_st[k], 1)
                for t in range(T):
                    dve.wait_ge(ln_st[k], t + 1)
                    v.bn_aggr(mv[:, t, :], st[:, t, :]).then_inc(ln_mv[k], 1)
                dve.wait_ge(ln_mv[k], T)
                v.tensor_scalar(veps[:], mv[:, :, 1], EPS, None, ALU.add).then_inc(ln_ve[k], 1)
                dve.wait_ge(ln_rs[k], 1)
                for t in range(T):
                    v.tensor_scalar(xn[k][:, t, :], src[:, t, :], mv[:, t, 0:1], rstd[:, t:t + 1],
                                    ALU.subtract, ALU.mult).then_inc(ln_xn[k], 1)

            def x_low(k):
                dve.wait_ge(xh_done[k], 1)
                v.tensor_tensor(xl[:], ps_m[BANK[(k, "xT", 0)]][:], xh[:].bitcast(F32), ALU.subtract
                                ).then_inc(xl_done[k], 1)

            def q_rest():
                dve.wait_ge(q1, 1)
                dve.wait_ge(xh_done["A"], 1)
                v.tensor_tensor(rest, ps_m[BANK[("A", "xT", 0)]][:], part(0), ALU.subtract).then_inc(q_r, 1)
                x_low("A")

            def q_part2():
                dve.wait_ge(q2, 1)
                v.tensor_tensor(part(2), rest, part(1), ALU.subtract).then_inc(q3, 1)

            def k_rest():
                dve.wait_ge(k1, 1)
                v.tensor_tensor(rest, rest, part(3), ALU.subtract).then_inc(k_r, 1)

            def k_part2():
                dve.wait_ge(k2, 1)
                v.tensor_tensor(part(5), rest, part(4), ALU.subtract).then_inc(k3, 1)

            def values_a():
                for t in range(T):
                    dve.wait_ge(v_ready, t + 1)
                    v.tensor_tensor(val[:, t], ps_m[BANK[("A", "V", t)]][:], bv_sb[:], ALU.add).then_inc(va, 1)

            def max_unit(k, g, n, beside):
                j, part_ = n // STAGES, n % STAGES
                u = g * STAGES * HG[k] + n
                if u >= 2:
                    dve.wait_ge(max_done[k], u - 1)
                elif k == "A" and beside:
                    dve.wait_ge(max_done["F"], UNITS["F"])
                dve.wait_ge(max_ready[k], u + 1)
                src = ps_max[u % 2]
                for t, c0 in (((3, 0),), ((1, 0), (0, 256)), ((2, 0),))[part_]:
                    w = (t + 1) * P
                    last = v.tensor_tensor_reduce(out=junk[:, u % 2, c0:c0 + w], in0=src[:, c0:c0 + w], in1=mask[:, S - w:S],
                                                  scale=1.0, scalar=NEG, op0=ALU.add, op1=ALU.max,
                                                  accum_out=mx[:, g % 2, 4 * j + t:4 * j + t + 1])
                last.then_inc(max_done[k], 1)

            def negate(k, g):
                c = 4 * HG[k]
                m, r = mx[:, g % 2, 0:c], nm_r[:, g % 2, 0:c]
                dve.wait_ge(max_done[k], (g + 1) * STAGES * HG[k])
                if g >= 2:
                    dve.wait_ge(t_ready[k], g - 1)
                if k == "A":
                    a = [nm_a[:, g % 2, 16 * n:16 * n + 16] for n in range(PARTS)]
                    v.tensor_scalar(a[0], m, -1.0, None, ALU.mult).then_inc(neg_step[k], 1)
                    dve.wait_ge(neg_step[k], 3 * g + 1)
                    v.scalar_tensor_tensor(out=r, in0=m, scalar=-1.0, in1=a[0], op0=ALU.mult, op1=ALU.subtract
                                           ).then_inc(neg_step[k], 1)
                    dve.wait_ge(neg_step[k], 3 * g + 2)
                    v.tensor_copy(a[1], r).then_inc(neg_step[k], 1)
                    dve.wait_ge(neg_step[k], 3 * g + 3)
                    v.tensor_tensor(a[2], r, a[1], ALU.subtract).then_inc(neg_ready[k], 1)
                else:
                    a = [nm_f[:, g % 2, 8 * n:8 * n + 8] for n in range(2)]
                    v.tensor_scalar(a[0].bitcast(F32R), m, -1.0, None, ALU.mult).then_inc(neg_step[k], 1)
                    dve.wait_ge(neg_step[k], g + 1)
                    v.scalar_tensor_tensor(out=a[1].bitcast(F32R), in0=m, scalar=-1.0, in1=a[0], op0=ALU.mult,
                                           op1=ALU.subtract).then_inc(neg_ready[k], 1)

            def inverse(k, g, j):
                w = S // HG[k]
                if j == 0:
                    dve.wait_ge(sums_out[k], g + 1)
                d = den[:, g % 2, j * w:j * w + w]
                v.reciprocal(d, d).then_inc(recip[k], 1)

            def divide(k, g):
                dve.wait_ge(recip[k], (g + 1) * HG[k])
                v.tensor_tensor(osb[:, g], osb[:, g], den[:, g % 2], ALU.mult).then_inc(o_done[k], 1)

            def outputs(phase, n):
                for u in OUTPUTS[phase, n]:
                    dve.wait_ge(sp_ready, u + 1)
                    if u >= 2:
                        dve.wait_ge(at_used, u - 1)
                    if u % E == 0:
                        dve.wait_ge(o_done["F"], u // E + 1)
                    v.tensor_tensor(at[:, u % 2], osb[:, u // E], ps_m[BANK[("F", "moe2", u)]][:], ALU.mult
                                    ).then_inc(at_done, 1)

            def outputs_end():
                dve.wait_ge(out_ready, 1)
                v.tensor_tensor(y_sb, ps_m[BANK[("F", "out", 0)]][:],
                                x1[:].rearrange("p t d -> p (t d)"), ALU.add).then_inc(y_done, 1)

            def attention(k, beside):
                n_units = STAGES * HG[k]
                for g in range(2):
                    for n in range(n_units):
                        max_unit(k, g, n, beside)
                        if k == "A" and beside:
                            outputs("pre", g * n_units + n)
                    negate(k, g)
                if k == "F" and beside:
                    q_rest()
                for g in range(GROUPS):
                    for s in range(STAGES):
                        n = g * STAGES + s
                        for j in range(HG[k]):
                            if g + 2 < GROUPS:
                                max_unit(k, g + 2, s * HG[k] + j, beside)
                            if k == "F" or beside:
                                outputs(k, n * HG[k] + j)
                            if s == 1 and g > 0:
                                inverse(k, g - 1, j)
                        if s == 1 and g > 0:
                            divide(k, g - 1)
                        if k == "F" and beside:
                            if n == 1:
                                q_part2()
                            elif n == 3:
                                k_rest()
                            elif n == 4:
                                k_part2()
                    if g + 2 < GROUPS:
                        negate(k, g + 2)
                if k == "A" and beside:
                    outputs_end()
                for j in range(HG[k]):
                    inverse(k, GROUPS - 1, j)
                divide(k, GROUPS - 1)

            def gate_ops():
                def step(n, ins):
                    ins.then_inc(gate_step, 1)

                def after(n):
                    dve.wait_ge(gate_step, n)
                dve.wait_ge(gate_exp, 1)
                step(1, v.tensor_scalar(g_w, g_s, 1.0, None, ALU.add))
                yield
                after(1)
                step(2, v.reciprocal(g_s, g_w))
                yield
                after(2)
                step(3, v.tensor_reduce(gmax[:], by_head(g_s), AX.X, ALU.max))
                yield
                after(3)
                step(4, v.tensor_tensor(by_head(g_w), by_head(g_s), gmax[:].unsqueeze(2).to_broadcast([P, T * 8, E]),
                                        ALU.is_ge))
                yield
                after(4)
                step(5, v.tensor_tensor(by_head(g_w), by_head(g_w), rank[:].unsqueeze(1).to_broadcast([P, T * 8, E]),
                                        ALU.mult))
                yield
                after(5)
                step(6, v.tensor_reduce(wmax[:], by_head(g_w), AX.X, ALU.max))
                yield
                after(6)
                step(7, v.tensor_tensor(by_head(hot), by_head(g_w), wmax[:].unsqueeze(2).to_broadcast([P, T * 8, E]),
                                        ALU.is_equal))
                yield
                after(7)
                step(8, v.tensor_tensor(g_m, g_s, hot, ALU.mult))
                yield

            def gates_halves():
                dve.wait_ge(gate_step, GS)
                gm = g_m.rearrange("p (t c) -> p t c", c=64)
                v.tensor_copy(g_t[:, :, 0:64].bitcast(F32R), gm).then_inc(gt_half, 1)
                dve.wait_ge(gt_half, 1)
                v.tensor_tensor(g_t[:, :, 64:128].bitcast(F32R), gm, g_t[:, :, 0:64], ALU.subtract
                                ).then_inc(gt_ready, 1)

            def experts():
                normalise("F", x1)
                x_low("F")
                gates = gate_ops()
                for u in range(8):
                    dve.wait_ge(qk_hi, u + 1)
                    hi = pt[:, 4 * (u // 2 % 2) + 2 * (u % 2)]
                    lo = pt[:, 4 * (u // 2 % 2) + 2 * (u % 2) + 1]
                    v.scalar_tensor_tensor(out=lo.bitcast(F32R), in0=ps_m[BANK[("F", "qk", u)]][:],
                                           scalar=(SCALE, 1.0)[u % 2], in1=hi, op0=ALU.mult, op1=ALU.subtract
                                           ).then_inc(qk_lo, 1)
                    next(gates)
                gates_halves()
                for t in range(T):
                    for e in range(E):
                        n = t * E + e
                        dve.wait_ge(moe1_ready, n + 1)
                        src = ps_m[BANK[("F", "moe1", n)]]
                        if e == 0:
                            v.tensor_copy(val[:, t], src[:]).then_inc(chosen, 1)
                        else:
                            dve.wait_ge(chosen, n)
                            pick = by_head(hot[:, t * 64:t * 64 + 64])[:, :, e:e + 1].to_broadcast([P, 8, 64])
                            v.copy_predicated(val[:, t].rearrange("p (h k) -> p h k", k=64), pick,
                                              src[:].rearrange("p (h k) -> p h k", k=64)).then_inc(chosen, 1)

            def first_layer():
                dve.wait_ge(w_ready, 1)
                dve.wait_ge(resid, 2)
                v.tensor_tensor(x1[:].rearrange("p t d -> p (t d)"), ps_m[BANK[("A", "W", 0)]][:],
                                x_sb[:].rearrange("p t d -> p (t d)"), ALU.add).then_inc(x1_done, 1)

            def low_half(n, hi, lo, raw):
                dve.wait_ge(split_hi, n + 1)
                v.tensor_tensor(lo[:], raw, hi[:].bitcast(F32), ALU.subtract).then_inc(split_lo, 1)

            def first():
                v.memset(ones[:], 1.0).then_inc(set_v, 1)
                v.memset(nm_f[:], 0.0).then_inc(set_v, 1)
                v.memset(mask[:], 0.0).then_inc(set_v, 1)
                for e in range(E):
                    v.memset(rank[:, e:e + 1], float(E - e))
                v.memset(s1q[:].bitcast(F32), 0.0).then_inc(set_v, 1)
                dve.wait_ge(x_in, 16)
                normalise("A", x_sb)
                dve.wait_ge(w_in[0], 16 * 4)
                v.tensor_copy(ident_b[:], ident_sb[:]).then_inc(set_v, 1)
                low_half(0, wk_h, wk_l, gflat[:, 0:128])
                low_half(1, wv_h, wv_l, gflat[:, 128:640])
                q_rest()
                q_part2()
                k_rest()
                k_part2()
                dve.wait_ge(w_in[1], 16 * 3)
                values_a()
                dve.wait_ge(w_in[2], 16 * 6)
                for n, (hi, lo, c0, c1) in enumerate(((wq_h, wq_l, 640, 1152), (wkf_h, wkf_l, 1152, 1664),
                                                      (wg_h, wg_l, 1664, 1728))):
                    low_half(2 + n, hi, lo, gflat[:, c0:c1])
                low_half(5, ve_h, ve_l, ve_raw)
                for p in range(4):
                    v.tensor_copy(spread[:].rearrange("r (p e) (a k) -> r p a e k", e=E, a=2)[:, p],
                                  ident2[:, 16 * p:16 * p + 16].rearrange("r (a e) -> r a e", a=2).unsqueeze(3)
                                  .to_broadcast([P, 2, E, 64]))
                attention("A", False)
                first_layer()

            def body(i):
                experts()
                dve.wait_ge(x_in, 16)
                normalise("A", x_sb)
                attention("F", True)
                values_a()
                outputs("gap", 0)
                attention("A", True)
                first_layer()

            def last(i):
                experts()
                attention("F", False)
                for phase, n in OUTPUTS:
                    if phase != "F":
                        outputs(phase, n)
                outputs_end()
            each_batch("dve", dve, first, body, last)


_NAMES = ["x", "wk", "bk", "wv", "bv", "wf", "bf", "wq", "wkf", "wg", "ve", "oe", "ident", "consts"]


def kernel(L0_attn_x, L0_attn_Wk, L0_attn_bk, L0_attn_Wv, L0_attn_bv, L0_attn_Wf, L0_attn_bf,
           L0_ffn_w_q, L0_ffn_w_k, L0_ffn_w_gate, L0_ffn_value_experts, L0_ffn_output_experts):
    import numpy as np
    import concourse.bacc as bacc
    from concourse.bass_utils import run_bass_kernel_spmd

    ve = np.transpose(np.asarray(L0_ffn_value_experts), (2, 0, 1, 3)).reshape(P, E * S)
    oe = np.asarray(L0_ffn_output_experts).reshape(E, 4, P, D).transpose(2, 1, 0, 3).reshape(P, 4 * E * D)
    wf = np.asarray(L0_attn_Wf).reshape(GROUPS, P, D).transpose(1, 0, 2).reshape(P, GROUPS * D)
    consts = np.ones((9, 4096), np.float32)
    consts[5:9] = 0.0
    consts[2:5] = np.full((3, 4096), 0x3F803F80, np.uint32).view(np.float32)
    values = [L0_attn_x, L0_attn_Wk, L0_attn_bk, L0_attn_Wv, L0_attn_bv, wf, L0_attn_bf, L0_ffn_w_q,
              L0_ffn_w_k, L0_ffn_w_gate, ve, oe, np.eye(P, dtype=np.float32), consts]
    nc = bacc.Bacc("TRN2", target_bir_lowering=False, num_devices=1)
    arrays, args = {}, []
    for name, a in zip(_NAMES, values):
        a = np.ascontiguousarray(a)
        arrays[f"in_{name}"] = a
        args.append(nc.dram_tensor(f"in_{name}", a.shape, mybir.dt.from_np(a.dtype), kind="ExternalInput").ap())
    out = nc.dram_tensor("out_0", (B, S, D), F32, kind="ExternalOutput").ap()
    build(nc, *args, out)
    r = run_bass_kernel_spmd(nc, [arrays], core_ids=[0])
    return r.results[0]["out_0"]
```

```python
import concourse.bass as bass
from concourse import mybir
from contextlib import ExitStack

F32 = mybir.dt.float32
F32R = mybir.dt.float32r
BF16 = mybir.dt.bfloat16
U32 = mybir.dt.uint32
ALU = mybir.AluOpType
ACT = mybir.ActivationFunctionType
AX = mybir.AxisListType

B, S, D = 8, 512, 128
P = 128
T = S // P
E = 8
HEADS = {"A": 16, "F": 8}
DV = {"A": 32, "F": 64}
GROUPS = 4
HG = {k: HEADS[k] // GROUPS for k in "AF"}
SPLIT_AT = 2
STAGES = 3
UNITS = {k: GROUPS * STAGES * HG[k] for k in "AF"}
NST = GROUPS * STAGES
DH = D // HEADS["A"]
SLICES = T
PARTS = 3
STACK = PARTS * PARTS * DH
KROWS = 96
NEG = -3.0e38
EPS = 1e-5
SCALE = 0.125
RESTACK = {"A": 2 * PARTS + 1, "F": 2}
SENDS = 12
WRITES = 2 * PARTS
MROWS = {"A": PARTS, "F": 2}

BANK = {("F", "xT", 0): 0, ("F", "gate", 0): 1, ("F", "gmT", 0): 1, ("A", "xT", 0): 0, ("A", "K", 0): 0,
        ("F", "acc", 0): 1, ("F", "out", 0): 0, ("A", "W", 0): 1}
BANK.update({("F", "qk", u): u % 2 for u in range(8)})
BANK.update({("F", "moe1", u): u % 4 for u in range(T * E)})
BANK.update({("F", "moe2", u): 0 for u in range(T * E)})
BANK.update({(k, "T", g): 0 for k in "AF" for g in range(GROUPS)})
BANK.update({("A", "V", t): 2 + t % 2 for t in range(T)})


VALUES = [(2 * p + t, e) for p in range(T // 2) for e in range(E) for t in range(2)]
VALUES_AT = {p: range(*r) for p, r in enumerate(((0, 0), (0, 12), (12, 22), (22, T * E)))}

MAX_FROM, TRANSPOSE_AT = 20, 29
N_MAX = 2 * STAGES * HG["F"]
MAX_AT = {MAX_FROM + n: range(N_MAX * n // (T * E - MAX_FROM), N_MAX * (n + 1) // (T * E - MAX_FROM))
          for n in range(T * E - MAX_FROM)}


def choices(n):
    return sum(e > 0 for t, e in VALUES[:n])


def place(phases):
    at, u = {}, 0
    for phase, steps, first, units in phases:
        at.update({(phase, n): [] for n in range(steps)})
        for m in range(units):
            at[phase, first + m * (steps - first) // units].append(u)
            u += 1
    assert u == T * E
    return at


FIRST_AT = 16
FIRST = {FIRST_AT + n: range(3 * n // 2, 3 * (n + 1) // 2) for n in range(8)}

OUTPUTS = place([("F", UNITS["F"], 14, 8), ("pre", STAGES * HG["A"], 0, 6), ("A", UNITS["A"], 0, 18)])


def build(nc, x, wk, bk, wv, bv, wf, bf, wq, wkf, wg, ve, oe, ident, consts, out):
    ctx = ExitStack()
    with ctx:
        def sb(name, shape, dt=F32):
            return ctx.enter_context(nc.sbuf_tensor(name, shape, dt))

        sems = []

        def sem(name):
            sems.append(ctx.enter_context(nc.semaphore(name)))
            return sems[-1]

        wk_h, wk_l = sb("wk_h", [P, D], F32R), sb("wk_l", [P, D], F32R)
        wv_h, wv_l = sb("wv_h", [P, S], F32R), sb("wv_l", [P, S], F32R)
        wq_h, wq_l = sb("wq_h", [P, S], F32R), sb("wq_l", [P, S], F32R)
        wkf_h, wkf_l = sb("wkf_h", [P, S], F32R), sb("wkf_l", [P, S], F32R)
        wg_h, wg_l = sb("wg_h", [P, 64], F32R), sb("wg_l", [P, 64], F32R)
        ve_h, ve_l = sb("ve_h", [P, E, S], F32R), sb("ve_l", [P, E, S], F32R)
        oe_sb = sb("oe_sb", [P, 4 * E, D])
        wf_sb = sb("wf_sb", [P, GROUPS, D])
        spread = sb("spread", [P, 4 * E, P], F32R)
        ident_sb = sb("ident_sb", [P, P])
        ident_b = sb("ident_b", [P, P], BF16)
        ident2 = sb("ident2", [P, 64])
        ones = sb("ones", [P, 64])
        mask = sb("mask", [P, S], BF16)
        bk_sb = sb("bk_sb", [P, 1])
        bv_sb = sb("bv_sb", [P, S])
        bf_sb = sb("bf_sb", [P, D])
        rank = sb("rank", [P, E])
        half = sb("half", [P, T])
        x_sb = sb("x_sb", [P, T, D])
        xn = {k: sb(f"xn{k}", [P, T, D]) for k in "AF"}
        x1 = sb("x1", [P, T, D])
        xh, xl = sb("xh", [P, S], F32R), sb("xl", [P, S], F32R)
        s1q, s1k = sb("s1q", [P, 8, S], F32R), sb("s1k", [P, 8, S], F32R)
        s2q, s2k = sb("s2q", [P, 8, S], F32R), sb("s2k", [P, 8, S], F32R)
        qs = s1q[:].rearrange("p a b -> p (a b)").bitcast(BF16).rearrange("p (h n) -> p h n", n=S)
        ks = s2k[:].rearrange("p a b -> p (a b)").bitcast(BF16).rearrange("p (h n) -> p h n", n=S)
        val = sb("val", [P, T, S])
        osb = sb("osb", [P, GROUPS, S])
        pt = sb("pt", [P, 8, S])
        at = sb("at", [P, 2, S])
        y_sb = at[:, 1]
        den = sb("den", [P, 2, S])
        gmt = sb("gmt", [P, S], F32R)
        junk = sb("junk", [P, 2, S], BF16)
        mx = sb("mx", [P, 2, 16])
        nm_r = sb("nm_r", [P, 2, 16])
        nm_a = sb("nm_a", [P, 2, 48], BF16)
        nm_f = sb("nm_f", [P, 2, 16])
        mt_a = sb("mt_a", [48, 2, P], BF16)
        mt_f = sb("mt_f", [16, 2, P])
        st = sb("st", [P, T, 6])
        mv = sb("mv", [P, T, 2])
        veps, rstd = sb("veps", [P, T]), sb("rstd", [P, T])
        gmax, wmax = sb("gmax", [P, T * 8]), sb("wmax", [P, T * 8])
        gflat = osb[:].rearrange("p a b -> p (a b)")
        g_s, g_w, g_m = gflat[:, 0:256], gflat[:, 256:512], gflat[:, 512:768]
        hot = gflat[:, 768:1024].bitcast(U32)
        g_t = gflat[:, 1024:1536].rearrange("p (t c) -> p t c", c=P)

        ve_raw = oe_sb[:].rearrange("p (e c) d -> p e (c d)", e=E)
        raw = {"wq": at[:, 0], "wkf": at[:, 1], "wg": xn["F"][:, 0, 0:64]}
        rest = pt[:, 7]

        def part(n):
            return pt[:, (2, 3, 6)[n // 2], :].bitcast(BF16)[:, (n % 2) * S:(n % 2) * S + S]

        def by_head(ap):
            return ap.rearrange("p (a e) -> p a e", e=E)

        def bank(name):
            return ctx.enter_context(nc.psum_tensor(name, [P, S], F32))
        ps_max = [bank("ps_max0"), bank("ps_max1")]
        ps_exp = [bank("ps_exp0"), bank("ps_exp1")]
        ps_o, ps_d = bank("ps_o"), bank("ps_d")
        ps_m = [bank("ps_m0"), bank("ps_m1")] + ps_exp

        parts_d = {n: nc.dram_tensor(f"parts_{n}", (PARTS, DH, HEADS["A"], S), BF16).ap() for n in "qk"}
        zeros_d = nc.dram_tensor("zeros_d", (4, 4096), F32).ap()
        ones_d = nc.dram_tensor("ones_d", (2, 4096), F32).ap()
        onesb_d = nc.dram_tensor("onesb_d", (PARTS, 8192), BF16).ap()

        w_in = [sem(f"w_in{n}") for n in range(3)]
        split_hi, split_lo = sem("split_hi"), sem("split_lo")
        oe_in = sem("oe_in")
        set_v, set_p = sem("set_v"), sem("set_p")
        cst = sem("cst")
        cleared = {n: sem(f"cleared_{n}") for n in ("sp", "pe", "act", "pool", "dve")}
        y_out = sem("y_out")
        first_of_batch = len(sems)
        arrived = sem("arrived")
        x_in = sem("x_in")
        K2 = lambda n: {k: sem(f"{n}{k}") for k in "AF"}
        ln_st, ln_mv, ln_ve, ln_rs, ln_xn = (K2(n) for n in ("ln_st", "ln_mv", "ln_ve", "ln_rs", "ln_xn"))
        xt_ready, xh_done, xl_done = K2("xt_ready"), K2("xh_done"), K2("xl_done")
        restacked = sem("restacked")
        restacked_a = [sem(f"restacked_a{g}") for g in range(GROUPS)]
        pair_sent = [sem("pair_sent0"), sem("pair_sent1")]
        max_ready, max_done = K2("max_ready"), K2("max_done")
        neg_step, neg_ready = K2("neg_step"), K2("neg_ready")
        t_ready, t_done = K2("t_ready"), K2("t_done")
        mrow = {k: [sem(f"mrow{k}{n}") for n in range(2)] for k in "AF"}
        s_ready, exp_done = K2("s_ready"), K2("exp_done")
        causal, pv_done, recip, o_done = K2("causal"), K2("pv_done"), K2("recip"), K2("o_done")
        den_out = K2("den_out")
        sums_out = K2("sums_out")
        q1, q_r, q2, q3 = sem("q1"), sem("q_r"), sem("q2"), sem("q3")
        k_ready, kf, k1, k_r, k2, k3 = (sem(n) for n in ("k_ready", "kf", "k1", "k_r", "k2", "k3"))
        parts_out = sem("parts_out")
        v_ready, va = sem("v_ready"), sem("va")
        resid = sem("resid")
        gelu_done, w_ready, x1_done = sem("gelu_done"), sem("w_ready"), sem("x1_done")
        gate_ready, gate_exp, gate_step, gt_ready, gmt_done = (
            sem(n) for n in ("gate_ready", "gate_exp", "gate_step", "gt_ready", "gmt_done"))
        gt_made, gt_half = sem("gt_made"), sem("gt_half")
        qk_ready, qk_hi, qk_lo = sem("qk_ready"), sem("qk_hi"), sem("qk_lo")
        moe1_ready, based, chosen, vf = (sem(n) for n in ("moe1_ready", "based", "chosen", "vf"))
        sp_ready, at_done, at_used = sem("sp_ready"), sem("at_done"), sem("at_used")
        acc_copied, out_ready, y_done = (sem(n) for n in ("acc_copied", "out_ready", "y_done"))

        numbers = [s.num for s in sems[first_of_batch:]]
        per_batch = range(numbers[0], numbers[-1] + 1)
        assert numbers == list(per_batch)

        block = ctx.enter_context(nc.Block())
        GS = 8

        def each_batch(name, eng, first, body, last):
            def meet():
                eng.drain().then_inc(arrived, 1)
                if name == "sp":
                    eng.wait_ge(arrived, 5)
                    eng.sem_clear(per_batch)
                    for go in cleared.values():
                        eng.sem_inc(go, 1)
                eng.wait_ge(cleared[name], 1)
                eng.sem_clear(cleared[name])
            first()
            meet()
            with eng.Fori(0, B - 1) as i:
                body(i)
                meet()
            last(B - 1)

        @block.sync
        def _(sp):
            o = gflat
            sp.dma_start(x_sb[:], x[0].rearrange("(t p) d -> p t d", p=P)).then_inc(x_in, 16)
            sp.dma_start(ident_sb[:], ident).then_inc(w_in[0], 16)
            sp.dma_start(o[:, 0:128], wk).then_inc(w_in[0], 16)
            sp.dma_start(o[:, 128:640], wv).then_inc(w_in[0], 16)
            sp.dma_start(bk_sb[:], bk.rearrange("(p o) -> p o", o=1)).then_inc(w_in[0], 16)
            sp.dma_start(zeros_d, consts[5:9]).then_inc(cst, 16)
            sp.dma_start(ones_d, consts[0:2]).then_inc(cst, 16)
            sp.dma_start(onesb_d, consts[2:5].bitcast(BF16)).then_inc(cst, 16)
            sp.wait_ge(cst, 16 * 3)
            sp.wait_ge(set_p, 3)
            sp.dma_start(ks[STACK:STACK + PARTS], onesb_d.rearrange("p (h n) -> p h n", n=S)).then_inc(cst, 16)
            sp.dma_start(bf_sb[:], bf.partition_broadcast(P)).then_inc(w_in[1], 16)
            sp.dma_start(bv_sb[:], bv.partition_broadcast(P)).then_inc(w_in[1], 16)
            sp.dma_start(wf_sb[:], wf.rearrange("p (g d) -> p g d", d=D)).then_inc(w_in[1], 16)
            sp.sem_inc(y_out, 16)

            def parts_to_dram(name):
                first_part, ready = {"q": (0, (q1, q2, q3)), "k": (PARTS, (k1, k2, k3))}[name]
                for m in range(PARTS):
                    sp.wait_ge(ready[m], 1)
                    sp.dma_start(parts_d[name][m].rearrange("d h n -> h d n"), part(first_part + m)
                                 ).then_inc(parts_out, 16)

            def restack_a(g):
                n_rows, h = PARTS * DH, slice(g * HG["A"], (g + 1) * HG["A"])
                for m in range(PARTS):
                    r = slice(m * n_rows, (m + 1) * n_rows)
                    sp.dma_start(ks[r, h], parts_d["k"].rearrange("m d h n -> (m d) h n")[:, h]
                                 ).then_inc(restacked_a[g], 16)
                    sp.dma_start(qs[r, h], parts_d["q"][m:m + 1, :, h].to_broadcast([PARTS, DH, HG["A"], S])
                                 ).then_inc(restacked_a[g], 16)
                sp.dma_start(qs[STACK:STACK + PARTS, h],
                             zeros_d[0:3].bitcast(BF16).rearrange("p (h n) -> p h n", n=S)[:, h]
                             ).then_inc(restacked_a[g], 16)

            def restack_f():
                sp.dma_start(s2q[64:66].bitcast(F32), zeros_d[0:2].rearrange("p (h n) -> p h n", n=S)
                             ).then_inc(restacked, 16)
                sp.dma_start(s2k[64:66].bitcast(F32), ones_d.rearrange("p (h n) -> p h n", n=S)
                             ).then_inc(restacked, 16)
                for p in range(4):
                    sp.wait_ge(qk_lo, 2 * p + 2)
                    qh, ql, kh, kl = (pt[:, 4 * (p % 2) + n, :] for n in range(4))
                    for ab in range(2):
                        r, h = slice(64 * ab, 64 * ab + 64), 2 * p + ab
                        for dst, src in ((s1q[0:64, h], qh), (s1q[64:128, h], ql), (s1k[0:64, h], kh),
                                         (s1k[64:128, h], kh), (s2q[0:64, h], qh), (s2k[0:64, h], kl)):
                            sp.dma_start(dst.bitcast(F32), src[r]).then_inc(pair_sent[p % 2], 16)

            def maxima_rows(k, g):
                sp.wait_ge(t_done[k], g + 1)
                for m in range(MROWS[k]):
                    if k == "A":
                        dst, src = qs[STACK + m:STACK + m + 1, 4 * g:4 * g + 4], mt_a[16 * m:16 * m + 16, g % 2]
                    else:
                        dst = s2q[64 + m:65 + m, 2 * g:2 * g + 2].bitcast(F32)
                        src = mt_f[8 * m:8 * m + 8, g % 2]
                    sp.dma_start(dst.rearrange("o h (t n) -> o (h t) n", n=P), src).then_inc(mrow[k][g % 2], 16)

            def attention_a():
                for g in range(GROUPS):
                    maxima_rows("A", g)

            def attention_f(next_batch):
                for g in range(GROUPS):
                    if next_batch and g >= 2:
                        parts_to_dram({2: "q", 3: "k"}[g])
                    maxima_rows("F", g)

            def store(i):
                sp.wait_ge(y_done, 1)
                dst = out[i] if isinstance(i, int) else out[bass.ds(i, 1)].rearrange("o s d -> (o s) d")
                sp.dma_start(dst.rearrange("(t p) d -> p t d", p=P), y_sb.rearrange("p (t d) -> p t d", d=D)).then_inc(y_out, 16)

            def store_landed():
                sp.wait_ge(y_out, 16)
                sp.sem_clear(y_out)

            def first():
                parts_to_dram("q")
                parts_to_dram("k")
                sp.wait_ge(parts_out, 16 * WRITES)
                for g in range(GROUPS):
                    restack_a(g)
                for dst, src in ((raw["wq"], wq), (raw["wkf"], wkf), (raw["wg"], wg), (ident2[0:64, :], ident[0:64, 0:64]), (ident2[64:128, :], ident[0:64, 0:64]),
                                 (ve_raw, ve.rearrange("p (e n) -> p e n", n=S))):
                    sp.dma_start(dst, src).then_inc(w_in[2], 16)
                attention_a()
                sp.wait_ge(split_hi, 6)
                sp.wait_ge(split_lo, 6)
                sp.dma_start(oe_sb[:], oe.rearrange("p (c d) -> p c d", d=D)).then_inc(oe_in, 16)

            def body(i):
                sp.dma_start(x_sb[:], x[bass.ds(i + 1, 1)].rearrange("o (t p) d -> p (o t) d", p=P)).then_inc(x_in, 16)
                restack_f()
                store_landed()
                attention_f(True)
                sp.wait_ge(parts_out, 16 * WRITES)
                for g in range(GROUPS):
                    sp.wait_ge(s_ready["F"], (g + 1) * STAGES * HG["F"])
                    restack_a(g)
                attention_a()
                store(i)

            def last(i):
                restack_f()
                store_landed()
                attention_f(False)
                store(i)
                sp.wait_ge(y_out, 16)
            each_batch("sp", sp, first, body, last)

        @block.tensor
        def _(pe):
            mm = nc.tensor.matmul

            def mm3(dst, lh, ll, rh, rl):
                mm(dst, lh, rh, start=True, stop=False)
                mm(dst, ll, rh, start=False, stop=False)
                return mm(dst, lh, rl, start=False, stop=True)

            def free(banks, k, name, n, drained):
                b = BANK[(k, name, n)]
                if banks[b] is not None:
                    pe.wait_ge(*banks[b])
                banks[b] = drained
                return ps_m[b]

            def transposed(banks, k):
                dst = free(banks, k, "xT", 0, (xl_done[k], 1))
                for t in range(T):
                    pe.wait_ge(ln_xn[k], t + 1)
                    last = nc.tensor.transpose(dst[:, t * P:t * P + P], xn[k][:, t, :], ident_sb[:])
                last.then_inc(xt_ready[k], 1)

            def keys_a(banks):
                pe.wait_ge(xl_done["A"], 1)
                dst = free(banks, "A", "K", 0, (kf, 1))
                mm3(dst[:], wk_h[:], wk_l[:], xh[:], xl[:]).then_inc(k_ready, 1)

            def values_a(banks, beside):
                if beside:
                    pe.wait_ge(exp_done["F"], UNITS["F"])
                for t in range(T):
                    dst = free(banks, "A", "V", t, (va, t + 1))
                    r = slice(t * P, t * P + P)
                    mm3(dst[:], xh[:, r], xl[:, r], wv_h[:], wv_l[:]).then_inc(v_ready, 1)

            def project_f(banks):
                transposed(banks, "F")
                pe.wait_ge(xl_done["F"], 1)
                dst = free(banks, "F", "gate", 0, (gate_exp, 1))
                for t in range(T):
                    r = slice(t * P, t * P + P)
                    last = mm3(dst[:, t * 64:t * 64 + 64], xh[:, r], xl[:, r], wg_h[:], wg_l[:])
                last.then_inc(gate_ready, 1)
                for u in range(8):
                    wh, wl = ((wq_h, wq_l), (wkf_h, wkf_l))[u % 2]
                    c = slice(u // 2 * P, u // 2 * P + P)
                    dst = free(banks, "F", "qk", u, (qk_lo, u + 1))
                    mm3(dst[:], wh[:, c], wl[:, c], xh[:], xl[:]).then_inc(qk_ready, 1)
                    if u % 2 == 1:
                        expert_values(banks, u // 2)
                    if u == 3:
                        gates_transposed(banks)

            def expert_values(banks, pair):
                for n in VALUES_AT[pair]:
                    t, e = VALUES[n]
                    r = slice(t * P, t * P + P)
                    dst = free(banks, "F", "moe1", n, (based, t + 1) if e == 0 else (chosen, choices(n + 1)))
                    mm3(dst[:], xh[:, r], xl[:, r], ve_h[:, e], ve_l[:, e]).then_inc(moe1_ready, 1)
                    for u in MAX_AT.get(n, ()):
                        if u == 0:
                            pe.wait_ge(restacked, 16 * RESTACK["F"])
                        g, m = divmod(u, STAGES * HG["F"])
                        if m == 0:
                            pe.wait_ge(pair_sent[g], 16 * SENDS)
                        max_unit("F", g, m, True)
                    if n == TRANSPOSE_AT:
                        maxima_transposed(banks, "F", 0)

            def gates_transposed(banks):
                dst = free(banks, "F", "gmT", 0, (gmt_done, 1))
                pe.wait_ge(gt_ready, 1)
                for t in range(T):
                    last = nc.tensor.transpose(dst[:, t * P:t * P + P], g_t[:, t, :], ident_sb[:])
                last.then_inc(gt_made, 1)

            def score(k, dst, h, rows, cols):
                (l1, l2), (r1, r2) = rows, cols
                if k == "A":
                    return mm(dst, l1[0:KROWS, h, l2], r1[0:KROWS, h, r2], start=True, stop=True)
                mm(dst, l1[0][:, h, l2], r1[0][:, h, r2], start=True, stop=False)
                return mm(dst, l1[1][0:KROWS, h, l2], r1[1][0:KROWS, h, r2], start=False, stop=True)

            Q = {"A": qs, "F": (s1q, s2q)}
            KK = {"A": ks, "F": (s1k, s2k)}

            def tile(n, m=1):
                return slice(n * P, (n + m) * P)

            def max_unit(k, g, n, beside):
                j, part_ = n // STAGES, n % STAGES
                h, u = g * HG[k] + j, g * STAGES * HG[k] + n
                if u >= 2:
                    pe.wait_ge(max_done[k], u - 1)
                elif k == "A" and beside:
                    pe.wait_ge(max_done["F"], UNITS["F"])
                dst = ps_max[u % 2]
                if part_ == 0:
                    last = score(k, dst[:], h, (Q[k], tile(3)), (KK[k], slice(0, S)))
                elif part_ == 1:
                    score(k, dst[:, 0:256], h, (Q[k], tile(1)), (KK[k], tile(0, 2)))
                    n0 = P if k == "A" else 2 * P
                    last = score(k, dst[:, 256:256 + n0], h, (Q[k], tile(0)), (KK[k], slice(0, n0)))
                else:
                    last = score(k, dst[:, 0:384], h, (Q[k], tile(2)), (KK[k], tile(0, 3)))
                last.then_inc(max_ready[k], 1)

            def maxima_transposed(banks, k, g):
                dst = free(banks, k, "T", g, (t_done[k], g + 1))
                pe.wait_ge(neg_ready[k], g + 1)
                if k == "A":
                    nc.tensor.transpose(dst[:].bitcast(BF16)[0:48, 0:P], nm_a[:, g % 2, :], ident_b[:]
                                        ).then_inc(t_ready[k], 1)
                else:
                    nc.tensor.transpose(dst[0:16, 0:P], nm_f[:, g % 2, :], ident_sb[:]).then_inc(t_ready[k], 1)

            def score_unit(k, g, s, j):
                u, h = (g * STAGES + s) * HG[k] + j, g * HG[k] + j
                if u >= 2:
                    pe.wait_ge(exp_done[k], u - 1)
                elif k == "A":
                    pe.wait_ge(va, T)
                else:
                    pe.wait_ge(chosen, choices(T * E))
                dst = ps_exp[u % 2]
                if s == 0:
                    last = score(k, dst[:], h, (KK[k], tile(0)), (Q[k], slice(0, S)))
                elif s == 1:
                    last = score(k, dst[:, 0:384], h, (KK[k], tile(1)), (Q[k], tile(1, 3)))
                else:
                    score(k, dst[:, 256:512], h, (KK[k], tile(2)), (Q[k], tile(2, 2)))
                    n0 = P if k == "A" else 2 * P
                    last = score(k, dst[:, 256 - n0:256], h, (KK[k], tile(3)), (Q[k], slice(S - n0, S)))
                last.then_inc(s_ready[k], 1)

            def weigh(k, n, beside):
                g, s, w = n // STAGES, n % STAGES, DV[k]
                pe.wait_ge(causal[k], n + 1)
                if s == 0:
                    if g > 0:
                        pe.wait_ge(sums_out[k], g)
                    elif k == "A" and beside:
                        pe.wait_ge(sums_out["F"], GROUPS)
                blocks = {0: [(0, 0, 0, S)], 1: [(1, 1, 0, 384)], 2: [(2, 2, P, 384), (3, 3, 0, P)]}[s]
                for dst, sums in ((ps_d, True), (ps_o, False)):
                    for kt, qt, c0, c1 in blocks:
                        for j in range(HG[k]):
                            h = g * HG[k] + j
                            left = ones[:, 0:w] if sums else val[:, kt, h * w:h * w + w]
                            last = mm(dst[j * w:j * w + w, qt * P:S], left,
                                      pt[:, (n % 2) * 4 + j, c0:c1], start=kt == 0, stop=kt == 3)
                last.then_inc(pv_done[k], 1)

            def product(u):
                pe.wait_ge(at_done, u + 1)
                mm(ps_m[1][:], oe_sb[:, u], at[:, u % 2], start=u == 0, stop=u == T * E - 1).then_inc(at_used, 1)

            def outputs(banks, phase, n):
                for u in OUTPUTS[phase, n]:
                    if u == 0:
                        free(banks, "F", "acc", 0, (acc_copied, 1))
                        pe.wait_ge(gmt_done, 1)
                    dst = free(banks, "F", "moe2", u, (at_done, u + 1))
                    mm(dst[:], spread[:, u], gmt[:], start=True, stop=True).then_inc(sp_ready, 1)
                    if u >= 1:
                        product(u - 1)

            def outputs_end(banks):
                product(T * E - 1)
                dst = free(banks, "F", "out", 0, (y_done, 1))
                pe.wait_ge(acc_copied, 1)
                for t in range(T):
                    last = nc.tensor.transpose(dst[:, t * P:t * P + P], at[:, 0, t * P:t * P + P], ident_sb[:])
                last.then_inc(out_ready, 1)

            def maxima_ahead(step):
                if step == FIRST_AT:
                    pe.wait_ge(restacked_a[0], 16 * RESTACK["A"])
                for n in FIRST.get(step, ()):
                    max_unit("A", 0, n, True)

            def attention(banks, k, beside):
                n_units = STAGES * HG[k]
                for g in range(2):
                    if k == "F" or g == 0 and beside:
                        continue
                    pe.wait_ge(restacked_a[g], 16 * RESTACK["A"])
                    for n in range(n_units):
                        max_unit(k, g, n, beside)
                        if beside:
                            outputs(banks, "pre", n)
                        if g == 1 and n == n_units // 2 - 1:
                            maxima_transposed(banks, k, 0)
                if k == "F" and beside:
                    transposed(banks, "A")
                for g in range(GROUPS):
                    if k == "F" and g + 2 < GROUPS:
                        pe.wait_ge(pair_sent[g], 2 * 16 * SENDS)
                    elif g + 2 < GROUPS:
                        pe.wait_ge(restacked_a[g + 2], 16 * RESTACK["A"])
                    pe.wait_ge(mrow[k][g % 2], 16 * MROWS[k] * (g // 2 + 1))
                    for s in range(STAGES):
                        n = g * STAGES + s
                        for j in range(HG[k]):
                            score_unit(k, g, s, j)
                            if g + 2 < GROUPS:
                                max_unit(k, g + 2, s * HG[k] + j, beside)
                            if k == "F" or beside:
                                outputs(banks, k, n * HG[k] + j)
                            if k == "F" and beside:
                                maxima_ahead(n * HG[k] + j)
                        if s == 0 and g + 1 < GROUPS:
                            maxima_transposed(banks, k, g + 1)
                        if n > 0:
                            if n == 1 and k == "F":
                                pe.wait_ge(vf, T)
                            weigh(k, n - 1, beside)
                        if n == 2 and k == "F" and beside:
                            keys_a(banks)
                weigh(k, NST - 1, beside)

            def project_back(banks):
                dst = free(banks, "A", "W", 0, (x1_done, 1))
                for g in range(GROUPS):
                    for t in range(T):
                        if g == 0 and t == 0:
                            pe.wait_ge(gelu_done, 1)
                        elif g == GROUPS - 1:
                            pe.wait_ge(gelu_done, 2 + t)
                        last = mm(dst[:, t * P:t * P + P], osb[:, g, t * P:t * P + P], wf_sb[:, g],
                                  start=g == 0 and t == 0, stop=g == GROUPS - 1 and t == T - 1)
                last.then_inc(w_ready, 1)

            def first():
                banks = [None] * 4
                pe.wait_ge(w_in[0], 16 * 4)
                transposed(banks, "A")
                pe.wait_ge(split_hi, 2)
                pe.wait_ge(split_lo, 2)
                keys_a(banks)
                values_a(banks, False)
                pe.wait_ge(cst, 16 * 4)
                pe.wait_ge(set_v, 5)
                pe.wait_ge(set_p, 4)
                attention(banks, "A", False)
                pe.wait_ge(w_in[1], 16 * 3)
                project_back(banks)
                pe.wait_ge(split_hi, 6)
                pe.wait_ge(split_lo, 6)
                pe.wait_ge(set_v, 6)
                pe.wait_ge(w_in[2], 16 * 6)
                pe.wait_ge(oe_in, 16)

            def experts(banks, next_batch):
                project_f(banks)
                attention(banks, "F", next_batch)

            def body(i):
                banks = [None] * 4
                experts(banks, True)
                values_a(banks, True)
                attention(banks, "A", True)
                outputs_end(banks)
                project_back(banks)

            def last(i):
                banks = [None] * 4
                experts(banks, False)
                for phase, n in OUTPUTS:
                    if phase != "F":
                        outputs(banks, phase, n)
                outputs_end(banks)
            each_batch("pe", pe, first, body, last)

        @block.scalar
        def _(act):
            copy = lambda dst, src: nc.scalar.activation(dst, src, ACT.Copy)

            def x_high(k):
                act.wait_ge(xt_ready[k], 1)
                copy(xh[:], ps_m[BANK[(k, "xT", 0)]][:]).then_inc(xh_done[k], 1)

            def q_part0():
                act.wait_ge(xt_ready["A"], 1)
                copy(part(0), ps_m[BANK[("A", "xT", 0)]][:]).then_inc(q1, 1)
                x_high("A")

            def q_part1():
                act.wait_ge(q_r, 1)
                copy(part(1), rest).then_inc(q2, 1)

            def k_part0():
                act.wait_ge(k_ready, 1)
                act.wait_ge(q3, 1)
                nc.scalar.activation(rest, ps_m[BANK[("A", "K", 0)]][:], ACT.Identity,
                                     bias=bk_sb[:, 0:1]).then_inc(kf, 1)
                act.wait_ge(kf, 1)
                copy(part(3), rest).then_inc(k1, 1)

            def k_part1():
                act.wait_ge(k_r, 1)
                copy(part(4), rest).then_inc(k2, 1)

            def maxima(k, g):
                act.wait_ge(t_ready[k], g + 1)
                src = ps_m[BANK[(k, "T", g)]]
                if g >= 2:
                    act.wait_ge(mrow[k][g % 2], 16 * MROWS[k])
                if k == "A":
                    copy(mt_a[:, g % 2, :], src[:].bitcast(BF16)[0:48, 0:P]).then_inc(t_done[k], 1)
                else:
                    copy(mt_f[:, g % 2, :], src[0:16, 0:P]).then_inc(t_done[k], 1)

            def sums(k, g, beside):
                act.wait_ge(pv_done[k], (g + 1) * STAGES)
                if g >= 2:
                    act.wait_ge(o_done[k], g - 1)
                if k == "A" and beside:
                    act.wait_ge(at_done, (g + 1) * E)
                copy(den[:, g % 2], ps_d[:]).then_inc(den_out[k], 1)
                copy(osb[:, g], ps_o[:]).then_inc(sums_out[k], 1)

            def attention(k, beside):
                maxima(k, 0)
                if k == "F":
                    for sent in pair_sent:
                        act.wait_ge(sent, 2 * 16 * SENDS)
                    if beside:
                        q_part0()
                for g in range(GROUPS):
                    if g == SPLIT_AT and k == "A" and not beside:
                        expert_weights_high()
                    for s in range(STAGES):
                        n = g * STAGES + s
                        if n >= 2:
                            act.wait_ge(pv_done[k], n - 1)
                        for j in range(HG[k]):
                            u = n * HG[k] + j
                            act.wait_ge(s_ready[k], u + 1)
                            c0, c1 = ((0, S), (0, 384), (P, S))[s]
                            nc.scalar.activation(pt[:, (n % 2) * 4 + j, 0:c1 - c0], ps_exp[u % 2][:, c0:c1],
                                                 ACT.Exp).then_inc(exp_done[k], 1)
                        if s == 0 and g + 1 < GROUPS:
                            maxima(k, g + 1)
                        if s == 0 and g > 0:
                            sums(k, g - 1, beside)
                        if k == "F" and beside:
                            if n == 0:
                                q_part1()
                            elif n == 2:
                                k_part0()
                            elif n == 3:
                                k_part1()
                sums(k, GROUPS - 1, beside)

            def gelu():
                g = GROUPS - 1
                for n, o in enumerate([osb[:, 0:g]] + [osb[:, g, t * P:(t + 1) * P] for t in range(T)]):
                    act.wait_ge(o_done["A"], g + n)
                    nc.scalar.activation(o, o, ACT.Gelu).then_inc(gelu_done, 1)

            def experts(next_batch):
                x_high("F")
                act.wait_ge(gate_ready, 1)
                nc.scalar.activation(g_s, ps_m[BANK[("F", "gate", 0)]][:, 0:256], ACT.Exp, scale=-1.0
                                     ).then_inc(gate_exp, 1)
                for u in range(8):
                    act.wait_ge(qk_ready, u + 1)
                    if u % 2 == 0 and u >= 4:
                        act.wait_ge(pair_sent[u // 2 % 2], 16 * SENDS)
                    nc.scalar.activation(pt[:, 4 * (u // 2 % 2) + 2 * (u % 2)].bitcast(F32R),
                                         ps_m[BANK[("F", "qk", u)]][:], ACT.Copy,
                                         scale=(SCALE, 1.0)[u % 2]).then_inc(qk_hi, 1)
                    if u % 2 == 1:
                        for n in VALUES_AT[u // 2]:
                            t, e = VALUES[n]
                            if e == 0:
                                act.wait_ge(moe1_ready, n + 1)
                                copy(val[:, t], ps_m[BANK[("F", "moe1", n)]][:]).then_inc(based, 1)
                    if u == 3:
                        act.wait_ge(gt_made, 1)
                        copy(gmt[:], ps_m[BANK[("F", "gmT", 0)]][:]).then_inc(gmt_done, 1)
                attention("F", next_batch)

            def outputs_end():
                act.wait_ge(at_used, T * E)
                copy(at[:, 0], ps_m[BANK[("F", "acc", 0)]][:]).then_inc(acc_copied, 1)

            def expert_weights_high():
                act.wait_ge(w_in[2], 16 * 6)
                for dst, name in ((wq_h, "wq"), (wkf_h, "wkf"), (wg_h, "wg")):
                    copy(dst[:], raw[name]).then_inc(split_hi, 1)
                copy(ve_h[:], ve_raw).then_inc(split_hi, 1)

            def first():
                act.wait_ge(w_in[0], 16 * 4)
                copy(wk_h[:], gflat[:, 0:128]).then_inc(split_hi, 1)
                copy(wv_h[:], gflat[:, 128:640]).then_inc(split_hi, 1)
                q_part0()
                q_part1()
                k_part0()
                k_part1()
                act.wait_ge(split_lo, 2)
                attention("A", False)
                gelu()

            def body(i):
                experts(True)
                attention("A", True)
                outputs_end()
                gelu()

            def last(i):
                experts(False)
                outputs_end()
            each_batch("act", act, first, body, last)

        @block.gpsimd
        def _(pool):
            tt = nc.gpsimd.tensor_tensor
            nc.gpsimd.memset(half[:], -0.5).then_inc(set_p, 1)

            def inverse_deviation(k):
                pool.wait_ge(ln_ve[k], 1)
                tt(rstd[:], veps[:], half[:], ALU.pow).then_inc(ln_rs[k], 1)

            def residual():
                pool.wait_ge(ln_xn["A"], T)
                tt(x_sb[:], x_sb[:], xn["A"][:], ALU.add).then_inc(resid, 1)
                pool.wait_ge(resid, 1)
                tt(x_sb[:], x_sb[:], bf_sb[:].unsqueeze(1).to_broadcast([P, T, D]), ALU.add).then_inc(resid, 1)

            def attention(k):
                for n in range(NST):
                    pool.wait_ge(exp_done[k], (n + 1) * HG[k])
                    s0, m = (n % 2) * 4, 2 if n % STAGES == 2 else 1
                    v = pt[:, s0:s0 + HG[k], 0:m * P].rearrange("p h (m c) -> p h m c", c=P)
                    nc.gpsimd.affine_select(out=v, in_=v, compare_op=ALU.is_ge, fill=0.0, base=0,
                                            pattern=[[0, HG[k]], [0, m], [1, P]], channel_multiplier=-1
                                            ).then_inc(causal[k], 1)

            def gated_values():
                for t in range(T):
                    pool.wait_ge(chosen, choices((t // 2 + 1) * 2 * E))
                    v = val[:, t].rearrange("p (h k) -> p h k", k=64)
                    tt(v, v, gmax[:, t * 8:t * 8 + 8].unsqueeze(2).to_broadcast([P, 8, 64]), ALU.mult
                       ).then_inc(vf, 1)

            def first():
                pool.wait_ge(set_p, 1)
                inverse_deviation("A")
                nc.gpsimd.memset(s2q[:].bitcast(F32), 0.0).then_inc(set_p, 1)
                nc.gpsimd.memset(s2k[:].bitcast(F32), 0.0).then_inc(set_p, 1)
                pool.wait_ge(set_v, 3)
                nc.gpsimd.affine_select(out=mask[:, S - P:S], in_=mask[:, S - P:S], compare_op=ALU.is_ge, fill=NEG,
                                        base=0, pattern=[[-1, P]], channel_multiplier=1).then_inc(set_p, 1)
                pool.wait_ge(w_in[1], 16 * 3)
                residual()
                attention("A")

            def experts(next_batch):
                inverse_deviation("F")
                if next_batch:
                    inverse_deviation("A")
                gated_values()

            def body(i):
                experts(True)
                attention("F")
                residual()
                attention("A")

            def last(i):
                experts(False)
                attention("F")
            each_batch("pool", pool, first, body, last)

        @block.vector
        def _(dve):
            v = nc.vector

            def statistics(k, src):
                for t in range(T):
                    v.bn_stats(st[:, t, :], src[:, t, :]).then_inc(ln_st[k], 1)
                for t in range(T):
                    dve.wait_ge(ln_st[k], t + 1)
                    v.bn_aggr(mv[:, t, :], st[:, t, :]).then_inc(ln_mv[k], 1)
                dve.wait_ge(ln_mv[k], T)
                v.tensor_scalar(veps[:], mv[:, :, 1], EPS, None, ALU.add).then_inc(ln_ve[k], 1)

            def normalise(k, src):
                dve.wait_ge(ln_rs[k], 1)
                for t in range(T):
                    v.tensor_scalar(xn[k][:, t, :], src[:, t, :], mv[:, t, 0:1], rstd[:, t:t + 1],
                                    ALU.subtract, ALU.mult).then_inc(ln_xn[k], 1)

            def x_low(k):
                dve.wait_ge(xh_done[k], 1)
                v.tensor_tensor(xl[:], ps_m[BANK[(k, "xT", 0)]][:], xh[:].bitcast(F32), ALU.subtract
                                ).then_inc(xl_done[k], 1)

            def q_rest():
                dve.wait_ge(q1, 1)
                dve.wait_ge(xh_done["A"], 1)
                v.tensor_tensor(rest, ps_m[BANK[("A", "xT", 0)]][:], part(0), ALU.subtract).then_inc(q_r, 1)
                x_low("A")

            def q_part2():
                dve.wait_ge(q2, 1)
                v.tensor_tensor(part(2), rest, part(1), ALU.subtract).then_inc(q3, 1)

            def k_rest():
                dve.wait_ge(k1, 1)
                v.tensor_tensor(rest, rest, part(3), ALU.subtract).then_inc(k_r, 1)

            def k_part2():
                dve.wait_ge(k2, 1)
                v.tensor_tensor(part(5), rest, part(4), ALU.subtract).then_inc(k3, 1)

            def values_a():
                for t in range(T):
                    dve.wait_ge(v_ready, t + 1)
                    v.tensor_tensor(val[:, t], ps_m[BANK[("A", "V", t)]][:], bv_sb[:], ALU.add).then_inc(va, 1)

            def max_unit(k, g, n, beside):
                j, part_ = n // STAGES, n % STAGES
                u = g * STAGES * HG[k] + n
                if u >= 2:
                    dve.wait_ge(max_done[k], u - 1)
                elif k == "A" and beside:
                    dve.wait_ge(max_done["F"], UNITS["F"])
                dve.wait_ge(max_ready[k], u + 1)
                src = ps_max[u % 2]
                for t, c0 in (((3, 0),), ((1, 0), (0, 256)), ((2, 0),))[part_]:
                    w = (t + 1) * P
                    last = v.tensor_tensor_reduce(out=junk[:, u % 2, c0:c0 + w], in0=src[:, c0:c0 + w], in1=mask[:, S - w:S],
                                                  scale=1.0, scalar=NEG, op0=ALU.add, op1=ALU.max,
                                                  accum_out=mx[:, g % 2, 4 * j + t:4 * j + t + 1])
                last.then_inc(max_done[k], 1)

            def negate(k, g):
                c = 4 * HG[k]
                m, r = mx[:, g % 2, 0:c], nm_r[:, g % 2, 0:c]
                dve.wait_ge(max_done[k], (g + 1) * STAGES * HG[k])
                if g >= 2:
                    dve.wait_ge(t_ready[k], g - 1)
                if k == "A":
                    a = [nm_a[:, g % 2, 16 * n:16 * n + 16] for n in range(PARTS)]
                    v.tensor_scalar(a[0], m, -1.0, None, ALU.mult).then_inc(neg_step[k], 1)
                    dve.wait_ge(neg_step[k], 3 * g + 1)
                    v.scalar_tensor_tensor(out=r, in0=m, scalar=-1.0, in1=a[0], op0=ALU.mult, op1=ALU.subtract
                                           ).then_inc(neg_step[k], 1)
                    dve.wait_ge(neg_step[k], 3 * g + 2)
                    v.tensor_copy(a[1], r).then_inc(neg_step[k], 1)
                    dve.wait_ge(neg_step[k], 3 * g + 3)
                    v.tensor_tensor(a[2], r, a[1], ALU.subtract).then_inc(neg_ready[k], 1)
                else:
                    a = [nm_f[:, g % 2, 8 * n:8 * n + 8] for n in range(2)]
                    v.tensor_scalar(a[0].bitcast(F32R), m, -1.0, None, ALU.mult).then_inc(neg_step[k], 1)
                    dve.wait_ge(neg_step[k], g + 1)
                    v.scalar_tensor_tensor(out=a[1].bitcast(F32R), in0=m, scalar=-1.0, in1=a[0], op0=ALU.mult,
                                           op1=ALU.subtract).then_inc(neg_ready[k], 1)

            def inverse(k, g, j):
                w = S // SLICES
                if j == 0:
                    dve.wait_ge(den_out[k], g + 1)
                d = den[:, g % 2, j * w:j * w + w]
                v.reciprocal(d, d).then_inc(recip[k], 1)

            def divide(k, g):
                dve.wait_ge(sums_out[k], g + 1)
                dve.wait_ge(recip[k], (g + 1) * SLICES)
                v.tensor_tensor(osb[:, g], osb[:, g], den[:, g % 2], ALU.mult).then_inc(o_done[k], 1)

            def outputs(phase, n):
                for u in OUTPUTS[phase, n]:
                    dve.wait_ge(sp_ready, u + 1)
                    if u >= 2:
                        dve.wait_ge(at_used, u - 1)
                    if u % E == 0:
                        dve.wait_ge(o_done["F"], u // E + 1)
                    v.tensor_tensor(at[:, u % 2], osb[:, u // E], ps_m[BANK[("F", "moe2", u)]][:], ALU.mult
                                    ).then_inc(at_done, 1)

            def outputs_end():
                dve.wait_ge(out_ready, 1)
                v.tensor_tensor(y_sb, ps_m[BANK[("F", "out", 0)]][:],
                                x1[:].rearrange("p t d -> p (t d)"), ALU.add).then_inc(y_done, 1)

            def attention(k, beside):
                n_units = STAGES * HG[k]
                for g in range(2):
                    if k == "F" or g == 0 and beside:
                        continue
                    for n in range(n_units):
                        max_unit(k, g, n, beside)
                        if k == "A" and beside:
                            outputs("pre", n)
                            if n % 2 == 1 and n // 2 < SLICES:
                                inverse("F", GROUPS - 1, n // 2)
                                if n // 2 == SLICES - 1:
                                    divide("F", GROUPS - 1)
                    negate(k, g)
                if k == "F" and beside:
                    q_rest()
                for g in range(GROUPS):
                    if g == SPLIT_AT and k == "A" and not beside:
                        expert_weights_low()
                    for s in range(STAGES):
                        n = g * STAGES + s
                        for j in range(HG[k]):
                            if g + 2 < GROUPS:
                                max_unit(k, g + 2, s * HG[k] + j, beside)
                            if k == "F" or beside:
                                outputs(k, n * HG[k] + j)
                            if k == "F" and beside:
                                for m in FIRST.get(n * HG[k] + j, ()):
                                    max_unit("A", 0, m, True)
                            slice_ = (s - 1) * HG[k] + j
                            if g > 0 and 0 <= slice_ < SLICES:
                                inverse(k, g - 1, slice_)
                                if slice_ == SLICES - 1:
                                    divide(k, g - 1)
                        if k == "F" and beside:
                            if n == 1:
                                q_part2()
                            elif n == 3:
                                k_rest()
                            elif n == 4:
                                k_part2()
                    if g + 2 < GROUPS:
                        negate(k, g + 2)
                g = GROUPS - 1
                if k == "A":
                    for j in range(SLICES):
                        inverse(k, g, j)
                        if j == 1 and beside:
                            outputs_end()
                        if j == 0:
                            dve.wait_ge(sums_out[k], g + 1)
                        dve.wait_ge(recip[k], g * SLICES + j + 1)
                        o = osb[:, g, j * P:(j + 1) * P]
                        v.tensor_tensor(o, o, den[:, g % 2, j * P:(j + 1) * P], ALU.mult).then_inc(o_done[k], 1)
                elif beside:
                    negate("A", 0)
                else:
                    for j in range(SLICES):
                        inverse(k, g, j)
                    divide(k, g)

            def gate_ops():
                def step(n, ins):
                    ins.then_inc(gate_step, 1)

                def after(n):
                    dve.wait_ge(gate_step, n)
                dve.wait_ge(gate_exp, 1)
                step(1, v.tensor_scalar(g_w, g_s, 1.0, None, ALU.add))
                yield
                after(1)
                step(2, v.reciprocal(g_s, g_w))
                yield
                after(2)
                step(3, v.tensor_reduce(gmax[:], by_head(g_s), AX.X, ALU.max))
                yield
                after(3)
                step(4, v.tensor_tensor(by_head(g_w), by_head(g_s), gmax[:].unsqueeze(2).to_broadcast([P, T * 8, E]),
                                        ALU.is_ge))
                yield
                after(4)
                step(5, v.tensor_tensor(by_head(g_w), by_head(g_w), rank[:].unsqueeze(1).to_broadcast([P, T * 8, E]),
                                        ALU.mult))
                yield
                after(5)
                step(6, v.tensor_reduce(wmax[:], by_head(g_w), AX.X, ALU.max))
                yield
                after(6)
                step(7, v.tensor_tensor(by_head(hot), by_head(g_w), wmax[:].unsqueeze(2).to_broadcast([P, T * 8, E]),
                                        ALU.is_equal))
                yield
                after(7)
                step(8, v.tensor_tensor(g_m, g_s, hot, ALU.mult))
                yield

            def gates_halves():
                dve.wait_ge(gate_step, GS)
                gm = g_m.rearrange("p (t c) -> p t c", c=64)
                v.tensor_copy(g_t[:, :, 0:64].bitcast(F32R), gm).then_inc(gt_half, 1)
                dve.wait_ge(gt_half, 1)
                v.tensor_tensor(g_t[:, :, 64:128].bitcast(F32R), gm, g_t[:, :, 0:64], ALU.subtract
                                ).then_inc(gt_ready, 1)

            def experts(next_batch):
                statistics("F", x1)
                normalise("F", x1)
                x_low("F")
                if next_batch:
                    dve.wait_ge(x_in, 16)
                    statistics("A", x_sb)
                    normalise("A", x_sb)
                gates = gate_ops()
                for u in range(8):
                    dve.wait_ge(qk_hi, u + 1)
                    hi = pt[:, 4 * (u // 2 % 2) + 2 * (u % 2)]
                    lo = pt[:, 4 * (u // 2 % 2) + 2 * (u % 2) + 1]
                    v.scalar_tensor_tensor(out=lo.bitcast(F32R), in0=ps_m[BANK[("F", "qk", u)]][:],
                                           scalar=(SCALE, 1.0)[u % 2], in1=hi, op0=ALU.mult, op1=ALU.subtract
                                           ).then_inc(qk_lo, 1)
                    if u < 4:
                        next(gates)
                        next(gates)
                    if u == 3:
                        gates_halves()
                    if u % 2 == 1:
                        expert_values(u // 2)

            def expert_values(pair):
                for n in VALUES_AT[pair]:
                    t, e = VALUES[n]
                    if e > 0:
                        dve.wait_ge(moe1_ready, n + 1)
                        dve.wait_ge(*((based, t + 1) if e == 1 else (chosen, choices(n - 1))))
                        pick = by_head(hot[:, t * 64:t * 64 + 64])[:, :, e:e + 1].to_broadcast([P, 8, 64])
                        v.copy_predicated(val[:, t].rearrange("p (h k) -> p h k", k=64), pick,
                                          ps_m[BANK[("F", "moe1", n)]][:].rearrange("p (h k) -> p h k", k=64)
                                          ).then_inc(chosen, 1)
                    for u in MAX_AT.get(n, ()):
                        g, m = divmod(u, STAGES * HG["F"])
                        max_unit("F", g, m, True)
                        if m == STAGES * HG["F"] - 1:
                            negate("F", g)

            def first_layer():
                dve.wait_ge(w_ready, 1)
                dve.wait_ge(resid, 2)
                v.tensor_tensor(x1[:].rearrange("p t d -> p (t d)"), ps_m[BANK[("A", "W", 0)]][:],
                                x_sb[:].rearrange("p t d -> p (t d)"), ALU.add).then_inc(x1_done, 1)

            def low_half(n, hi, lo, raw):
                dve.wait_ge(split_hi, n + 1)
                v.tensor_tensor(lo[:], raw, hi[:].bitcast(F32), ALU.subtract).then_inc(split_lo, 1)

            def expert_weights_low():
                dve.wait_ge(w_in[2], 16 * 6)
                for n, (hi, lo, name) in enumerate(((wq_h, wq_l, "wq"), (wkf_h, wkf_l, "wkf"), (wg_h, wg_l, "wg"))):
                    low_half(2 + n, hi, lo, raw[name])
                low_half(5, ve_h, ve_l, ve_raw)
                for p in range(4):
                    last = v.tensor_copy(spread[:].rearrange("r (p e) (a k) -> r p a e k", e=E, a=2)[:, p],
                                         ident2[:, 16 * p:16 * p + 16].rearrange("r (a e) -> r a e", a=2).unsqueeze(3)
                                         .to_broadcast([P, 2, E, 64]))
                last.then_inc(set_v, 1)

            def first():
                v.memset(ones[:], 1.0).then_inc(set_v, 1)
                v.memset(nm_f[:], 0.0).then_inc(set_v, 1)
                v.memset(mask[:], 0.0).then_inc(set_v, 1)
                for e in range(E):
                    v.memset(rank[:, e:e + 1], float(E - e))
                v.memset(s1q[:].bitcast(F32), 0.0).then_inc(set_v, 1)
                dve.wait_ge(x_in, 16)
                statistics("A", x_sb)
                normalise("A", x_sb)
                dve.wait_ge(w_in[0], 16 * 4)
                v.tensor_copy(ident_b[:], ident_sb[:]).then_inc(set_v, 1)
                low_half(0, wk_h, wk_l, gflat[:, 0:128])
                low_half(1, wv_h, wv_l, gflat[:, 128:640])
                q_rest()
                q_part2()
                k_rest()
                k_part2()
                dve.wait_ge(w_in[1], 16 * 3)
                values_a()
                attention("A", False)
                first_layer()

            def body(i):
                experts(True)
                attention("F", True)
                values_a()
                attention("A", True)
                first_layer()

            def last(i):
                experts(False)
                attention("F", False)
                for phase, n in OUTPUTS:
                    if phase != "F":
                        outputs(phase, n)
                outputs_end()
            each_batch("dve", dve, first, body, last)


_NAMES = ["x", "wk", "bk", "wv", "bv", "wf", "bf", "wq", "wkf", "wg", "ve", "oe", "ident", "consts"]


def kernel(L0_attn_x, L0_attn_Wk, L0_attn_bk, L0_attn_Wv, L0_attn_bv, L0_attn_Wf, L0_attn_bf,
           L0_ffn_w_q, L0_ffn_w_k, L0_ffn_w_gate, L0_ffn_value_experts, L0_ffn_output_experts):
    import numpy as np
    import concourse.bacc as bacc
    from concourse.bass_utils import run_bass_kernel_spmd

    ve = np.transpose(np.asarray(L0_ffn_value_experts), (2, 0, 1, 3)).reshape(P, E * S)
    oe = np.asarray(L0_ffn_output_experts).reshape(E, 4, P, D).transpose(2, 1, 0, 3).reshape(P, 4 * E * D)
    wf = np.asarray(L0_attn_Wf).reshape(GROUPS, P, D).transpose(1, 0, 2).reshape(P, GROUPS * D)
    consts = np.ones((9, 4096), np.float32)
    consts[5:9] = 0.0
    consts[2:5] = np.full((3, 4096), 0x3F803F80, np.uint32).view(np.float32)
    values = [L0_attn_x, L0_attn_Wk, L0_attn_bk, L0_attn_Wv, L0_attn_bv, wf, L0_attn_bf, L0_ffn_w_q,
              L0_ffn_w_k, L0_ffn_w_gate, ve, oe, np.eye(P, dtype=np.float32), consts]
    nc = bacc.Bacc("TRN2", target_bir_lowering=False, num_devices=1)
    arrays, args = {}, []
    for name, a in zip(_NAMES, values):
        a = np.ascontiguousarray(a)
        arrays[f"in_{name}"] = a
        args.append(nc.dram_tensor(f"in_{name}", a.shape, mybir.dt.from_np(a.dtype), kind="ExternalInput").ap())
    out = nc.dram_tensor("out_0", (B, S, D), F32, kind="ExternalOutput").ap()
    build(nc, *args, out)
    r = run_bass_kernel_spmd(nc, [arrays], core_ids=[0])
    return r.results[0]["out_0"]
```
